# Optimizing a Trainium2 kernel written in Bass

```python
import numpy as np
import jax
import jax.numpy as jnp

def _softmax(x, axis=-1):
    return jax.nn.softmax(x, axis=axis)

def _gelu(x):
    return jax.nn.gelu(x, approximate=True)

def _silu(x):
    return jax.nn.silu(x)

def _sigmoid(x):
    return jax.nn.sigmoid(x)

def _layernorm(x, axis=-1, eps=1e-05):
    m = jnp.mean(x, axis=axis, keepdims=True)
    v = jnp.var(x, axis=axis, keepdims=True)
    return (x - m) / jnp.sqrt(v + eps)

def _scatter_add(tgt, idx, src, axis=0):
    return tgt.at[idx].add(src)

def _segment_sum(src, seg, n):
    return jax.ops.segment_sum(src, seg, n)
kernel_name = 'mk_lm_tower_d1_tok_ids1024_r4_55c895'

def setup_inputs(seed: int=0):
    np.random.seed(seed)
    _w = jnp.asarray

    def _rec_inputs():
        import jax
        import jax.numpy as jnp
        _rk = jax.random.key(seed)
        x = jax.random.randint(jax.random.fold_in(_rk, 1), (2, 2048), 0, 12564, jnp.int32)
        return x
    x = _rec_inputs()

    def _L0_tok_setup():
        import jax, jax.numpy as jnp
        import numpy as np
        SCALING = 16.0 / 8.0
        key = jax.random.key(seed)
        k1, k2, k3, k4 = jax.random.split(key, 4)
        vocab, dim, rank = (50257, 256, 8)
        x = jax.random.randint(k1, (8, 512), 0, vocab, dtype=jnp.int64)
        base_weight = jax.random.normal(k2, (vocab, dim), dtype=jnp.float32)
        lora_A = jax.random.normal(k3, (vocab, rank), dtype=jnp.float32) * 0.01
        lora_B = jax.random.normal(k4, (rank, dim), dtype=jnp.float32)
        return {'x': x, 'base_weight': base_weight, 'lora_A': lora_A, 'lora_B': lora_B}
    _L0_tok_all = _L0_tok_setup()
    _L0_tok_in = {k: v for k, v in _L0_tok_all.items() if k in ('base_weight', 'lora_A', 'lora_B')}
    del _L0_tok_all

    def _L0_attn_setup():
        import jax, jax.numpy as jnp
        import numpy as np
        CHUNK = 64
        NORM_EPS = 1e-05
        DENOM_EPS = 1.0
        B, S, HID, H = (4, 1024, 256, 8)
        D = HID // H

        def rmsnorm(x, w, eps=NORM_EPS):
            var = jnp.mean(x * x, axis=-1, keepdims=True)
            return x * jax.lax.rsqrt(var + eps) * w

        def chunked_linear_attn(q, k, v):
            b, s, h, d = q.shape
            n = s // CHUNK

            def to_chunks(x):
                return x.reshape(b, n, CHUNK, h, d).transpose(1, 0, 3, 2, 4)
            qc, kc, vc = (to_chunks(q), to_chunks(k), to_chunks(v))
            mask = jnp.tril(jnp.ones((CHUNK, CHUNK), dtype=q.dtype))

            def step(state, inp):
                qq, kk, vv = inp
                inter = jnp.einsum('bhcd,bhde->bhce', qq, state)
                scores = jnp.einsum('bhcd,bhed->bhce', qq, kk) * mask
                intra = jnp.einsum('bhce,bhed->bhcd', scores, vv)
                state = state + jnp.einsum('bhcd,bhce->bhde', kk, vv)
                return (state, inter + intra)
            init = jnp.zeros((b, h, d, d), dtype=q.dtype)
            _, o = jax.lax.scan(step, init, (qc, kc, vc))
            return o.transpose(1, 0, 3, 2, 4).reshape(b, s, h, d)
        key = jax.random.key(seed)
        k0, k1, k2, k3, k4 = jax.random.split(key, 5)
        hidden_states = jax.random.normal(k0, (B, S, HID), dtype=jnp.float32)
        Wq = jax.random.normal(k1, (HID, HID), dtype=jnp.float32) * 0.02
        Wk = jax.random.normal(k2, (HID, HID), dtype=jnp.float32) * 0.02
        Wv = jax.random.normal(k3, (HID, HID), dtype=jnp.float32) * 0.02
        Wo = jax.random.normal(k4, (HID, HID), dtype=jnp.float32) * 0.02
        norm_w = jnp.ones((D,), dtype=jnp.float32)
        return {'hidden_states': hidden_states, 'Wq': Wq, 'Wk': Wk, 'Wv': Wv, 'Wo': Wo, 'norm_w': norm_w}
    _L0_attn_all = _L0_attn_setup()
    _L0_attn_in = {k: v for k, v in _L0_attn_all.items() if k in ('Wq', 'Wk', 'Wv', 'Wo', 'norm_w')}
    del _L0_attn_all

    def _L0_ffn_setup():
        import jax, jax.numpy as jnp
        import numpy as np
        BLOCK = 32
        W_BITS = 4
        ACT_BITS = 16

        def act_qdq(x):
            qmax = 2.0 ** (ACT_BITS - 1) - 1.0
            scale = jnp.maximum(jnp.max(jnp.abs(x)) / qmax, 1e-12)
            return jnp.clip(jnp.round(x / scale), -qmax - 1.0, qmax) * scale

        def fixed_qdq_u16(x):
            scale = 1.0 / 65536.0
            return jnp.clip(jnp.round(x / scale), 0.0, 65535.0) * scale

        def lpbq_dequant(w):
            O, I = w.shape
            qmax = 2.0 ** (W_BITS - 1) - 1.0
            wb = w.reshape(O, I // BLOCK, BLOCK)
            s = jnp.maximum(jnp.max(jnp.abs(wb), axis=-1, keepdims=True) / qmax, 1e-12)
            wq = jnp.clip(jnp.round(wb / s), -qmax - 1.0, qmax) * s
            return wq.reshape(O, I)
        key = jax.random.key(seed)
        k1, k2, k3, k4 = jax.random.split(key, 4)
        B, S, H, I = (2, 1024, 256, 768)
        x = jax.random.normal(k1, (B, S, H), jnp.float32)
        w_gate = jax.random.normal(k2, (I, H), jnp.float32) * 0.02
        w_up = jax.random.normal(k3, (I, H), jnp.float32) * 0.02
        w_down = jax.random.normal(k4, (H, I), jnp.float32) * 0.02
        return {'x': x, 'w_gate': w_gate, 'w_up': w_up, 'w_down': w_down}
    _L0_ffn_all = _L0_ffn_setup()
    _L0_ffn_in = {k: v for k, v in _L0_ffn_all.items() if k in ('w_gate', 'w_up', 'w_down')}
    del _L0_ffn_all
    return {'x': x, 'L0_tok_base_weight': _L0_tok_in['base_weight'], 'L0_tok_lora_A': _L0_tok_in['lora_A'], 'L0_tok_lora_B': _L0_tok_in['lora_B'], 'L0_attn_Wq': _L0_attn_in['Wq'], 'L0_attn_Wk': _L0_attn_in['Wk'], 'L0_attn_Wv': _L0_attn_in['Wv'], 'L0_attn_Wo': _L0_attn_in['Wo'], 'L0_attn_norm_w': _L0_attn_in['norm_w'], 'L0_ffn_w_gate': _L0_ffn_in['w_gate'], 'L0_ffn_w_up': _L0_ffn_in['w_up'], 'L0_ffn_w_down': _L0_ffn_in['w_down']}

def reference(x, L0_tok_base_weight, L0_tok_lora_A, L0_tok_lora_B, L0_attn_Wq, L0_attn_Wk, L0_attn_Wv, L0_attn_Wo, L0_attn_norm_w, L0_ffn_w_gate, L0_ffn_w_up, L0_ffn_w_down):
    import jax
    import jax.numpy as jnp

    def _L0_tok_ref(x, base_weight, lora_A, lora_B):
        import jax, jax.numpy as jnp
        import numpy as np
        SCALING = 16.0 / 8.0
        h = base_weight[x]
        after_A = lora_A[x]
        return h + jnp.einsum('bsr,rd->bsd', after_A, lora_B) * SCALING

    def _L0_attn_ref(hidden_states, Wq, Wk, Wv, Wo, norm_w):
        import jax, jax.numpy as jnp
        import numpy as np
        CHUNK = 64
        NORM_EPS = 1e-05
        DENOM_EPS = 1.0
        B, S, HID, H = (4, 1024, 256, 8)
        D = HID // H

        def rmsnorm(x, w, eps=NORM_EPS):
            var = jnp.mean(x * x, axis=-1, keepdims=True)
            return x * jax.lax.rsqrt(var + eps) * w

        def chunked_linear_attn(q, k, v):
            b, s, h, d = q.shape
            n = s // CHUNK

            def to_chunks(x):
                return x.reshape(b, n, CHUNK, h, d).transpose(1, 0, 3, 2, 4)
            qc, kc, vc = (to_chunks(q), to_chunks(k), to_chunks(v))
            mask = jnp.tril(jnp.ones((CHUNK, CHUNK), dtype=q.dtype))

            def step(state, inp):
                qq, kk, vv = inp
                inter = jnp.einsum('bhcd,bhde->bhce', qq, state)
                scores = jnp.einsum('bhcd,bhed->bhce', qq, kk) * mask
                intra = jnp.einsum('bhce,bhed->bhcd', scores, vv)
                state = state + jnp.einsum('bhcd,bhce->bhde', kk, vv)
                return (state, inter + intra)
            init = jnp.zeros((b, h, d, d), dtype=q.dtype)
            _, o = jax.lax.scan(step, init, (qc, kc, vc))
            return o.transpose(1, 0, 3, 2, 4).reshape(b, s, h, d)
        b, s, _ = hidden_states.shape
        q = jnp.einsum('bsd,ed->bse', hidden_states, Wq).reshape(b, s, H, D)
        k = jnp.einsum('bsd,ed->bse', hidden_states, Wk).reshape(b, s, H, D)
        v = jnp.einsum('bsd,ed->bse', hidden_states, Wv).reshape(b, s, H, D)
        o = chunked_linear_attn(q, k, v)
        z = jnp.cumsum(k, axis=1)
        denom = jnp.maximum(jnp.abs(jnp.sum(q * z, axis=-1)), DENOM_EPS)[..., None]
        o = o / denom
        o = rmsnorm(o, norm_w)
        o = o.reshape(b, s, H * D)
        return jnp.einsum('bse,de->bsd', o, Wo)

    def _L0_ffn_ref(x, w_gate, w_up, w_down):
        import jax, jax.numpy as jnp
        import numpy as np
        BLOCK = 32
        W_BITS = 4
        ACT_BITS = 16

        def act_qdq(x):
            qmax = 2.0 ** (ACT_BITS - 1) - 1.0
            scale = jnp.maximum(jnp.max(jnp.abs(x)) / qmax, 1e-12)
            return jnp.clip(jnp.round(x / scale), -qmax - 1.0, qmax) * scale

        def fixed_qdq_u16(x):
            scale = 1.0 / 65536.0
            return jnp.clip(jnp.round(x / scale), 0.0, 65535.0) * scale

        def lpbq_dequant(w):
            O, I = w.shape
            qmax = 2.0 ** (W_BITS - 1) - 1.0
            wb = w.reshape(O, I // BLOCK, BLOCK)
            s = jnp.maximum(jnp.max(jnp.abs(wb), axis=-1, keepdims=True) / qmax, 1e-12)
            wq = jnp.clip(jnp.round(wb / s), -qmax - 1.0, qmax) * s
            return wq.reshape(O, I)
        x = act_qdq(x)
        up = act_qdq(x @ lpbq_dequant(w_up).T)
        gate = act_qdq(x @ lpbq_dequant(w_gate).T)
        sig = fixed_qdq_u16(jax.nn.sigmoid(gate))
        gate = act_qdq(gate * sig)
        o = act_qdq(gate * up)
        return o @ lpbq_dequant(w_down).T
    h = _L0_tok_ref(x, L0_tok_base_weight, L0_tok_lora_A, L0_tok_lora_B)
    h = h + _L0_attn_ref(_layernorm(h, axis=-1), L0_attn_Wq, L0_attn_Wk, L0_attn_Wv, L0_attn_Wo, L0_attn_norm_w)
    h = h + _L0_ffn_ref(_layernorm(h, axis=-1), L0_ffn_w_gate, L0_ffn_w_up, L0_ffn_w_down)
    return h

_drawn_inputs = setup_inputs


def setup_inputs(seed=0):
    import zlib

    import numpy as np

    out = dict(_drawn_inputs(seed))
    spreads = {'L0_attn_norm_w': (1.0, 0.2)}
    factors = {}
    for name, (base, spread) in spreads.items():
        noise = np.random.default_rng([zlib.crc32(name.encode()), seed]).standard_normal(out[name].shape)
        drawn = base * np.exp(spread * noise) if base else spread * noise
        out[name] = jnp.asarray(drawn.astype(out[name].dtype))
    for name, factor in factors.items():
        out[name] = (out[name] * factor).astype(out[name].dtype)
    return out
```

```python
from contextlib import ExitStack

import concourse.bass as bass
from concourse import mybir

ALU = mybir.AluOpType
ACT = mybir.ActivationFunctionType
AX = mybir.AxisListType
F32 = mybir.dt.float32
F16 = mybir.dt.float16
I16 = mybir.dt.int16
U16 = mybir.dt.uint16
I32 = mybir.dt.int32

P = 128
NORM_EPS = 1e-5
LORA_SCALING = 2.0
QMAX_ACT = 2.0**15 - 1.0
QMAX_W = 2.0**3 - 1.0
QMAX_SIG = 65535.0
SIG_STEPS = 65536.0
MIN_SCALE = 1e-12
QBLOCK = 32
ROUNDER = 12582912.0


def lm_tower(nc, x, base, lora_a, lora_b, wq, wk, wv, wo, norm_w, w_gate, w_up, w_down, out):
    B, S = x.shape
    D = base.shape[1]
    R = lora_a.shape[1]
    DH = norm_w.shape[0]
    H = D // DH
    FF = w_gate.shape[0]
    TILES = B * S // P
    CHUNKS = S // P
    KD = D // P
    MF = FF // P
    HG = P // DH
    NG = H // HG
    DV = DH + 1
    SW = HG * DV
    GT = 4
    GW = GT * P
    GROUPS = TILES // GT
    GF = MF * GW
    HALF = GF // 2
    OT = D // P
    assert B == 2 and KD == 2 and NG == 2 and MF % 3 == 0 and TILES % GT == 0 and R <= 32

    h2_dram = nc.dram_tensor("h2_kept", (TILES, P, D), F32, kind="Internal").ap()

    with ExitStack() as ctx:
        def sb(name, shape, dt=F32):
            return ctx.enter_context(nc.sbuf_tensor(name, shape, dt))

        def sem(name):
            return ctx.enter_context(nc.semaphore(name))

        big = sb("big", [P, GROUPS * GF])
        quant = sb("quant", [P, GROUPS * GF], I16)
        xregion = sb("xregion", [P, 2 * KD * TILES * P], F16)
        ident = sb("ident", [P, P])
        ones = sb("ones", [P, P])
        minus_half = sb("minus_half", [P, H])
        up_hi = sb("up_hi", [P, KD, FF], F16)
        up_lo = sb("up_lo", [P, KD, FF], F16)
        gate_hi = sb("gate_hi", [P, KD, FF], F16)
        gate_lo = sb("gate_lo", [P, KD, FF], F16)
        down_hi = sb("down_hi", [P, MF, D], F16)
        down_lo = sb("down_lo", [P, MF, D], F16)
        absmax = sb("absmax", [P, GROUPS * MF])
        maxima = sb("maxima", [P, 4])
        top = sb("top", [P, 4])
        pick = sb("pick", [P, 4])
        scales = sb("scales", [P, 32])
        idx = sb("idx", [P, TILES], I32)
        idx_slot = sb("idx_slot", [P, GT], I32)
        stats6 = sb("stats6", [P, 2, 6])
        meanvar = sb("meanvar", [P, 2, 2, 2])
        vareps = sb("vareps", [P, 2, 2])
        rstd = sb("rstd", [P, 2, 2])
        ssq = sb("ssq", [P, H])
        denom2 = sb("denom2", [P, H])
        meansq = sb("meansq", [P, 2, H])
        onorm = sb("onorm", [P, 2, H])

        big_at = [0]

        def in_big(shape):
            n = 1
            for k in shape:
                n *= k
            v = big[:, big_at[0]:big_at[0] + n]
            big_at[0] += n
            assert big_at[0] <= GROUPS * GF
            names = "abcd"[:len(shape)]
            if len(shape) == 1:
                return v
            return v.rearrange(f"p ({' '.join(names)}) -> p {' '.join(names)}",
                               **{c: k for c, k in zip(names[1:], shape[1:])})

        h_all = in_big([TILES, D])
        base_ring = in_big([GT, D])
        lora_ring = in_big([GT, R])
        lora_t = in_big([2, P])
        xn = in_big([2, D])
        xn_t = in_big([2, KD, P])
        qk_ring = in_big([GT, 2 * D])
        v_ring = in_big([GT, H, DV])
        qkt_ring = in_big([GT, 2 * NG, P])
        probs = in_big([2, HG, NG, P])
        state = in_big([B, NG, SW])
        state_new = in_big([2, NG, SW])
        diag = in_big([NG, SW])
        squares = in_big([2, H, DV])
        o_n = in_big([2, D])
        o_t = in_big([2, KD, P])
        xn2 = in_big([2, D])

        xreg32 = xregion[:].bitcast(F32)
        x_at = [0]

        def in_x(n):
            v = xreg32[:, x_at[0]:x_at[0] + n]
            x_at[0] += n
            assert x_at[0] <= KD * TILES * P
            return v

        wqkv_t = in_x(KD * 3 * D).rearrange("p (k n) -> p k n", k=KD)
        wo_t = in_x(KD * D).rearrange("p (k n) -> p k n", k=KD)
        lora_b2 = in_x(D)
        causal = in_x(2 * NG * P)
        norm_col = in_x(1)
        ffn_nat = in_x(3 * KD * FF)
        quant32 = quant[:].bitcast(F32)
        xn2_t = quant32[:, 0:KD * TILES * P].rearrange("p (k n) -> p k n", k=KD)
        attn_nat = quant32[:, KD * TILES * P:KD * TILES * P + 4 * KD * D].rearrange(
            "p (w k n) -> p w k n", w=4, k=KD)
        x16 = quant[:, 2 * KD * TILES * P:2 * KD * TILES * P + 2 * KD * GW].rearrange(
            "p (s k n) -> p s k n", s=2, k=KD)
        NBLK = 3 * KD * FF // QBLOCK
        blk = big[:, big_at[0]:big_at[0] + 3 * NBLK].rearrange("p (a b) -> p a b", a=3)
        idx_rows = big[0:TILES, big_at[0] + 3 * NBLK:big_at[0] + 3 * NBLK + P]
        idx_raw = big[0:TILES, big_at[0] + 3 * NBLK + P:big_at[0] + 3 * NBLK + 2 * P].bitcast(I32)

        xh = xregion[:, 0:KD * TILES * P].rearrange("p (k n) -> p k n", k=KD)
        xl = xregion[:, KD * TILES * P:2 * KD * TILES * P].rearrange("p (k n) -> p k n", k=KD)
        g16 = xregion[:, 0:2 * HALF].bitcast(I16).rearrange("p (s n) -> p s n", s=2)
        sig16 = xregion[:, 2 * HALF:4 * HALF].bitcast(U16).rearrange("p (s n) -> p s n", s=2)
        sig = xregion[:, 4 * HALF:8 * HALF].bitcast(F32).rearrange("p (s n) -> p s n", s=2)
        oh = xregion[:, 0:2 * GF].rearrange("p (s m n) -> p s m n", s=2, m=MF)
        ol = xregion[:, 2 * GF:4 * GF].rearrange("p (s m n) -> p s m n", s=2, m=MF)
        res = xregion[:, 4 * GF:4 * GF + 4 * GT * D].bitcast(F32).rearrange(
            "p (s t d) -> p s t d", s=2, t=GT)
        o16 = sb("o16", [P, GF], I16)

        scores_ps = ctx.enter_context(nc.psum_tensor("scores_ps", [P, HG, 512], F32))
        qk_bank = ctx.enter_context(nc.psum_tensor("qk_bank", [P, 512], F32))
        vws_bank = ctx.enter_context(nc.psum_tensor("vws_bank", [P, 512], F32))
        lo_bank = ctx.enter_context(nc.psum_tensor("lo_bank", [P, 512], F32))
        turn_bank = ctx.enter_context(nc.psum_tensor("turn_bank", [P, 512], F32))
        banks = [scores_ps[:, n, :] for n in range(HG)] + [qk_bank[:], vws_bank[:], lo_bank[:], turn_bank[:]]

        x_loaded = sem("x_loaded")
        attn_w_loaded = sem("attn_w_loaded")
        ffn_w_loaded = sem("ffn_w_loaded")
        ident_ready = sem("ident_ready")
        consts_ready = sem("consts_ready")
        pool_chain = sem("pool_chain")
        idx_rows_ready = sem("idx_rows_ready")
        idx_turned = sem("idx_turned")
        idx_ready = sem("idx_ready")
        lora_b_ready = sem("lora_b_ready")
        attn_w_turned = sem("attn_w_turned")
        qkv_w_ready = sem("qkv_w_ready")
        wo_ready = sem("wo_ready")
        ffn_w_quantised = sem("ffn_w_quantised")
        ffn_w_turned = sem("ffn_w_turned")
        ffn_w_hi = sem("ffn_w_hi")
        ffn_w_lo = sem("ffn_w_lo")
        dve_chain = sem("dve_chain")
        maxima_ready = sem("maxima_ready")
        maxima_turned = sem("maxima_turned")
        pick_ready = sem("pick_ready")
        top_spread = sem("top_spread")
        scale_ready = sem("scale_ready")
        slot_ready = sem("slot_ready")
        gathered = [sem(f"gathered{n}") for n in range(GT)]
        lora_turned = sem("lora_turned")
        lora_t_ready = sem("lora_t_ready")
        lora_done = sem("lora_done")
        h_ready = sem("h_ready")
        stats_done = sem("stats_done")
        meanvar_done = sem("meanvar_done")
        vareps_ready = sem("vareps_ready")
        rstd_ready = sem("rstd_ready")
        xn_ready = sem("xn_ready")
        xn_turned = sem("xn_turned")
        xn_t_ready = sem("xn_t_ready")
        qk_done = sem("qk_done")
        qk_ready = sem("qk_ready")
        v_done = sem("v_done")
        v_ready = sem("v_ready")
        qk_turned = sem("qk_turned")
        qkt_ready = sem("qkt_ready")
        scores_done = sem("scores_done")
        probs_ready = sem("probs_ready")
        o_done = sem("o_done")
        squares_ready = sem("squares_ready")
        ssq_done = sem("ssq_done")
        denom2_done = sem("denom2_done")
        meansq_ready = sem("meansq_ready")
        onorm_ready = sem("onorm_ready")
        o_n_ready = sem("o_n_ready")
        o_turned = sem("o_turned")
        o_t_ready = sem("o_t_ready")
        state_done = sem("state_done")
        state_masked = sem("state_masked")
        state_ready = sem("state_ready")
        attn_done = sem("attn_done")
        h2_ready = sem("h2_ready")
        h2_stored = [sem(f"h2_stored{n}") for n in range(GT)]
        stats2_done = sem("stats2_done")
        meanvar2_done = sem("meanvar2_done")
        vareps2_ready = sem("vareps2_ready")
        rstd2_ready = sem("rstd2_ready")
        xn2_ready = sem("xn2_ready")
        xn2_turned = sem("xn2_turned")
        xn2_t_ready = sem("xn2_t_ready")
        absmax_ready = sem("absmax_ready")
        x16_ready = sem("x16_ready")
        xh_ready = sem("xh_ready")
        xl_ready = sem("xl_ready")
        up_done = sem("up_done")
        up_kept = sem("up_kept")
        up_max = sem("up_max")
        up_quantised = sem("up_quantised")
        gate_done = sem("gate_done")
        gate_kept = sem("gate_kept")
        gate_max = sem("gate_max")
        gate_quantised = sem("gate_quantised")
        sig_ready = sem("sig_ready")
        sig_quantised = sem("sig_quantised")
        silu_ready = sem("silu_ready")
        silu_max = sem("silu_max")
        silu_quantised = sem("silu_quantised")
        prod_ready = sem("prod_ready")
        prod_max = sem("prod_max")
        o16_ready = sem("o16_ready")
        oh_ready = sem("oh_ready")
        ol_ready = sem("ol_ready")
        down_done = sem("down_done")
        res_loaded = [sem(f"res_loaded{n}") for n in range(2)]
        out_ready = sem("out_ready")
        out_stored = [sem(f"out_stored{n}") for n in range(2)]

        def fixed(n):
            return isinstance(n, int)

        def at(start, n):
            return slice(start, start + n) if fixed(start) else bass.ds(start, n)

        def due(g, c):
            return not fixed(g) or 0 <= GT * g + c < TILES

        def tile_wait(eng, s, g, c, per=1):
            if not fixed(g):
                eng.wait_ge(s, g * (GT * per) + (c + 1) * per)
            elif GT * g + c >= 0:
                eng.wait_ge(s, min(GT * g + c + 1, TILES) * per)

        def slot_wait(eng, s, g, c, per):
            eng.wait_ge(s, g * per + (c // GT + 1) * per)

        def hold_on_constant(eng):
            eng.wait_ge(consts_ready, 1)

        def run_pipeline(eng, iteration):
            for i in range(-2, GT):
                iteration(i // GT, i % GT)
            with eng.Fori(1, TILES // GT - 1) as g:
                for u in range(GT):
                    iteration(g, u)
            for i in range(TILES - GT, TILES + 4):
                iteration(i // GT, i % GT)

        def run_groups(eng, group, n):
            group(0)
            with eng.Fori(1, n) as k:
                group(k)

        def w_part(n, low):
            which, k = n // 3, 2 * (n % 3)
            if which == 2:
                return (down_hi, down_lo)[low][:, k:k + 2, :]
            return ((up_hi, up_lo), (gate_hi, gate_lo))[which][low][:, :, k * P:(k + 2) * P]

        def w_bank(n):
            return banks[(4 + n) % 7].rearrange("p (k n) -> p k n", k=2)

        block = ctx.enter_context(nc.Block())

        (S_X, C_X, S_UP, C_UP, S_GATE, C_GATE, S_SILU, C_SILU, S_PROD, C_PROD, S_OUT, S_SIG,
         T0, T1) = (scales[:, n:n + 1] for n in range(14))
        EXP = scales[:, 14:17].bitcast(I32)
        TO_F16 = scales[:, 17:20]
        FROM_F16 = scales[:, 20:23]

        @block.sync
        def _(sp):
            sp.dma_start(idx_raw, x.rearrange("b (c p) -> (b c) p", p=P)).then_inc(x_loaded, 16)
            sp.dma_start(lora_b2[0:R, :], lora_b).then_inc(attn_w_loaded, 16)
            for n, w in enumerate((wq, wk, wv, wo)):
                sp.dma_start(attn_nat[:, n], w.rearrange("(k p) n -> p k n", p=P)).then_inc(attn_w_loaded, 16)
            for r in range(HG):
                sp.dma_start(norm_col[r * DH:(r + 1) * DH, :],
                             norm_w.rearrange("(d o) -> d o", o=1)).then_inc(attn_w_loaded, 16)
            for n, w in enumerate((w_up, w_gate, w_down)):
                width = KD * FF
                sp.dma_start(ffn_nat[:, n * width:(n + 1) * width].rearrange("p (k n) -> p k n", n=w.shape[1]),
                             w.rearrange("(k p) n -> p k n", p=P)).then_inc(ffn_w_loaded, 16)

            def iteration(g, u):
                c = u - 3
                if due(g, c):
                    tile_wait(sp, h2_ready, g, c)
                    sp.dma_start(h2_dram[at(g * GT + c, 1)].rearrange("o p d -> p (o d)"),
                                 h_all[:, at(g * GT + c, 1), :].rearrange("p o d -> p (o d)")
                                 ).then_inc(h2_stored[c % GT], 16)

            run_pipeline(sp, iteration)
            for n in range(GT):
                sp.wait_ge(h2_stored[n], 16 * (TILES // GT))

            out_v = out.rearrange("b (c p) d -> b p c d", p=P)

            def load(pair, s):
                sp.dma_start(res[:, s], h2_dram[at(pair * 2 * GT + s * GT, GT)].rearrange("t p d -> p t d")
                             ).then_inc(res_loaded[s], 16)

            def store(pair, s):
                for b in range(B):
                    sp.dma_start(out_v[b, :, at(pair * 4 + s * 2, 2), :],
                                 res[:, s].rearrange("p (c b) d -> p b c d", b=B)[:, b]
                                 ).then_inc(out_stored[s], 16)

            sp.wait_ge(prod_max, 2 * GROUPS)
            load(0, 0)
            load(0, 1)

            def pair_of_groups(q):
                for s in range(2):
                    sp.wait_ge(out_ready, q * (2 * GT) + (s + 1) * GT)
                    store(q, s)
                for s in range(2):
                    sp.wait_ge(out_stored[s], q * 32 + 32)
                    load(q + 1, s)

            with sp.Fori(0, GROUPS // 2 - 1) as q:
                pair_of_groups(q)
            last = GROUPS // 2 - 1
            for s in range(2):
                sp.wait_ge(out_ready, last * 2 * GT + (s + 1) * GT)
                store(last, s)
            for s in range(2):
                sp.wait_ge(out_stored[s], 32 * (GROUPS // 2))

        @block.gpsimd
        def _(pool):
            chain = [0]

            def link(ins):
                chain[0] += 1
                ins.then_inc(pool_chain, 1)
                pool.wait_ge(pool_chain, chain[0])

            link(pool.memset(ident[:], 0.0))
            pool.affine_select(out=ident[:], in_=ident[:], compare_op=ALU.not_equal, fill=1.0, base=0,
                               pattern=[[-1, P]], channel_multiplier=1).then_inc(ident_ready, 1)
            link(pool.memset(ones[:], 1.0))
            link(pool.memset(minus_half[:], -0.5))
            link(pool.memset(causal, 1.0))
            link(pool.affine_select(out=causal.rearrange("p (n t) -> p n t", t=P),
                                    in_=causal.rearrange("p (n t) -> p n t", t=P),
                                    compare_op=ALU.is_ge, fill=0.0, base=0, pattern=[[0, 2 * NG], [1, P]],
                                    channel_multiplier=-1))
            link(pool.memset(diag, 0.0))
            for r in range(HG):
                link(pool.memset(diag[r * DH:(r + 1) * DH, :, r * DV:(r + 1) * DV], 1.0))
            link(pool.memset(state, 0.0))
            pool.memset(v_ring, 1.0).then_inc(consts_ready, 1)

            def gather(n):
                for dst, table in ((base_ring, base), (lora_ring, lora_a)):
                    pool.indirect_dma_start(
                        dst[:, n], None, table,
                        bass.IndirectOffsetOnAxis(ap=idx_slot[:, n:n + 1], axis=0)).then_inc(gathered[n], 16)

            pool.wait_ge(idx_ready, 1)
            pool.tensor_copy(idx_slot[:], idx[:, 0:GT]).then_inc(slot_ready, GT)
            pool.wait_ge(slot_ready, GT)
            for n in range(GT):
                gather(n)

            def iteration(g, u):
                fetch = due(g, u) and due(g, u + GT)
                if fetch:
                    hold_on_constant(pool)
                    tile_wait(pool, h_ready, g, u)
                    tile_wait(pool, lora_turned, g, u)
                    pool.tensor_copy(idx_slot[:, u:u + 1], idx[:, at(g * GT + u + GT, 1)]).then_inc(slot_ready, 1)
                c = u + 1
                if due(g, c):
                    tile_wait(pool, vareps_ready, g, c)
                    if fetch:
                        tile_wait(pool, slot_ready, g, u + GT)
                    pool.tensor_tensor(rstd[:, c % 2, 0:1], vareps[:, c % 2, 0:1], minus_half[:, 0:1],
                                       ALU.pow).then_inc(rstd_ready, 1)
                if fetch:
                    gather(u)
                c = u - 3
                if due(g, c):
                    tile_wait(pool, vareps2_ready, g, c)
                    pool.tensor_tensor(rstd[:, c % 2, 1:2], vareps[:, c % 2, 1:2], minus_half[:, 0:1],
                                       ALU.pow).then_inc(rstd2_ready, 1)
                c = u - 2
                if due(g, c):
                    tile_wait(pool, meansq_ready, g, c)
                    pool.tensor_tensor(onorm[:, c % 2], meansq[:, c % 2], minus_half[:], ALU.pow
                                       ).then_inc(onorm_ready, 1)
                    tile_wait(pool, state_masked, g, c)
                    pool.tensor_tensor(state[:, c % B], state[:, c % B], state_new[:, c % 2], ALU.add
                                       ).then_inc(state_ready, 1)

            run_pipeline(pool, iteration)

        @block.scalar
        def _(act):
            def copy(dst, src, scale=1.0):
                return act.activation(dst, src, ACT.Copy, scale=scale)

            for n in range(3):
                act.wait_ge(attn_w_turned, n + 1)
                copy(wqkv_t[:, :, n * D:(n + 1) * D], banks[n].rearrange("p (k n) -> p k n", k=KD)
                     ).then_inc(qkv_w_ready, 1)
            for n in range(9):
                act.wait_ge(ffn_w_turned, n + 1)
                copy(w_part(n, 0), w_bank(n)).then_inc(ffn_w_hi, 1)
            act.wait_ge(consts_ready, 1)

            def iteration(g, u):
                c = u
                if due(g, c):
                    tile_wait(act, qk_done, g, c)
                    copy(qk_ring[:, c % GT], qk_bank[:]).then_inc(qk_ready, 1)
                c = u - 3
                if due(g, c):
                    tile_wait(act, o_turned, g, c)
                    copy(o_t[:, c % 2], turn_bank[:, 0:KD * P].rearrange("p (k n) -> p k n", k=KD)
                         ).then_inc(o_t_ready, 1)
                c = u
                if due(g, c):
                    tile_wait(act, qk_turned, g, c)
                    copy(qkt_ring[:, c % GT], qk_bank[:].rearrange("p (k n) -> p k n", k=2 * NG)
                         ).then_inc(qkt_ready, 1)
                c = u - 4
                if due(g, c):
                    hold_on_constant(act)
                    tile_wait(act, xn2_turned, g, c)
                    copy(xn2_t[:, :, at((g * GT + c) * P, P)],
                         turn_bank[:, 0:KD * P].rearrange("p (k n) -> p k n", k=KD)).then_inc(xn2_t_ready, 1)
                c = u - 2
                if due(g, c):
                    tile_wait(act, o_done, g, c)
                    act.activation(squares[:, c % 2], lo_bank[:, 0:H * DV].rearrange(
                        "p (h d) -> p h d", h=H), ACT.Square).then_inc(squares_ready, 1)
                c = u + 1
                if due(g, c):
                    tile_wait(act, xn_turned, g, c)
                    copy(xn_t[:, c % 2], turn_bank[:, 0:KD * P].rearrange("p (k n) -> p k n", k=KD)
                         ).then_inc(xn_t_ready, 1)
                c = u + 2
                if due(g, c):
                    tile_wait(act, lora_turned, g, c)
                    copy(lora_t[0:R, c % 2], turn_bank[0:R, KD * P:KD * P + P]).then_inc(lora_t_ready, 1)

            run_pipeline(act, iteration)

            act.wait_ge(scale_ready, 1)

            def quantise_x(n, s):
                hold_on_constant(act)
                if not fixed(n) or n >= 2:
                    act.wait_ge(xl_ready, n - 1)
                copy(x16[:, s], xn2_t[:, :, at(n * GW, GW)], C_X).then_inc(x16_ready, 1)
                hold_on_constant(act)
                act.wait_ge(x16_ready, n + 1)
                copy(xh[:, :, at(n * GW, GW)], x16[:, s]).then_inc(xh_ready, 1)

            quantise_x(0, 0)
            quantise_x(1, 1)
            with act.Fori(1, GROUPS // 2) as q:
                for s in range(2):
                    quantise_x(q * 2 + s, s)

            def keep(name_done, name_kept, also=None):
                def group(n):
                    if also is not None:
                        act.wait_ge(also, n + 1)
                    for m in range(MF):
                        hold_on_constant(act)
                        act.wait_ge(name_done, n * MF + m + 1)
                        copy(big[:, at(n * GF + m * GW, GW)], banks[m]).then_inc(name_kept, 1)
                return group

            for n in range(GT):
                act.wait_ge(h2_stored[n], 16 * (TILES // GT))
            run_groups(act, keep(up_done, up_kept), GROUPS)
            run_groups(act, keep(gate_done, gate_kept, up_quantised), GROUPS)

            act.wait_ge(scale_ready, 3)

            def gate_pass(q):
                for s in range(2):
                    hold_on_constant(act)
                    if not fixed(q) or q >= 1:
                        act.wait_ge(silu_ready, q * 2 + (s - 1))
                    copy(g16[:, s], big[:, at(q * GF + s * HALF, HALF)], C_GATE).then_inc(gate_quantised, 1)
                    if not fixed(q) or q >= 1:
                        act.wait_ge(sig_quantised, q * 2 + (s - 1))
                    act.wait_ge(gate_quantised, q * 2 + (s + 1))
                    act.activation(sig[:, s], g16[:, s], ACT.Sigmoid, scale=S_GATE).then_inc(sig_ready, 1)

            run_groups(act, gate_pass, GROUPS)

            act.wait_ge(scale_ready, 4)

            def silu_pass(q):
                for s in range(2):
                    hold_on_constant(act)
                    if not fixed(q) or q >= 1:
                        act.wait_ge(prod_ready, q * 2 + (s - 1))
                    copy(g16[:, s], big[:, at(q * GF + s * HALF, HALF)], C_SILU).then_inc(silu_quantised, 1)

            run_groups(act, silu_pass, GROUPS)

            act.wait_ge(scale_ready, 5)

            def product_parts(q):
                for s in range(2):
                    hold_on_constant(act)
                    if s or not fixed(q) or q >= 1:
                        act.wait_ge(ol_ready, q * 2 + s)
                    copy(o16[:], big[:, at(q * 2 * GF + s * GF, GF)], C_PROD).then_inc(o16_ready, 1)
                    if not fixed(q) or q >= 1:
                        act.wait_ge(down_done, q * (2 * GT) + (s - 1) * GT)
                    act.wait_ge(o16_ready, q * 2 + (s + 1))
                    copy(oh[:, s], o16[:].rearrange("p (m n) -> p m n", m=MF)).then_inc(oh_ready, 1)

            run_groups(act, product_parts, GROUPS // 2)


        @block.vector
        def _(dve):
            chain = [0]

            def link(ins):
                chain[0] += 1
                ins.then_inc(dve_chain, 1)
                dve.wait_ge(dve_chain, chain[0])

            barriers = [0]

            def spread_maxima(n, parts):
                parts().then_inc(maxima_ready, 1)
                barriers[0] += 1
                dve.wait_ge(maxima_turned, barriers[0])
                link(dve.tensor_reduce(top[0:n, 0:1], turn_bank[0:n, 0:P], AX.X, ALU.max))
                dve.tensor_scalar(pick[0:n, 0:n], ident[0:n, 0:n], top[0:n, 0:1], None, ALU.mult
                                  ).then_inc(pick_ready, 1)
                dve.wait_ge(top_spread, barriers[0])
                return turn_bank[:, 0:n]

            def scale_of(largest, units, scale, inverse):
                if units is None:
                    link(dve.tensor_scalar(scale, largest, 1.0 / QMAX_ACT, MIN_SCALE, ALU.mult, ALU.max))
                    dve.reciprocal(inverse, scale).then_inc(scale_ready, 1)
                    return
                link(dve.tensor_scalar(T0, largest, units, 1.0 / QMAX_ACT, ALU.mult, ALU.mult))
                link(dve.tensor_scalar(scale, T0, MIN_SCALE, None, ALU.max))
                link(dve.reciprocal(T1, scale))
                dve.tensor_scalar(inverse, T1, units, None, ALU.mult).then_inc(scale_ready, 1)

            dve.wait_ge(x_loaded, 16)
            dve.tensor_copy(idx_rows, idx_raw).then_inc(idx_rows_ready, 1)
            dve.wait_ge(idx_turned, 1)
            dve.tensor_copy(idx[:].rearrange("p (c b) -> p b c", b=B),
                            turn_bank[:, 0:TILES].rearrange("p (b c) -> p b c", b=B)).then_inc(idx_ready, 1)

            dve.wait_ge(attn_w_loaded, 16 * (1 + 4 + HG))
            dve.tensor_scalar(lora_b2[0:R, :], lora_b2[0:R, :], LORA_SCALING, None, ALU.mult
                              ).then_inc(lora_b_ready, 1)
            dve.wait_ge(attn_w_turned, 4)
            dve.tensor_scalar(wo_t, banks[3].rearrange("p (k n) -> p k n", k=KD), norm_col, None, ALU.mult
                              ).then_inc(wo_ready, 1)

            dve.wait_ge(ffn_w_loaded, 16 * 3)
            blocks = ffn_nat.rearrange("p (b q) -> p b q", q=QBLOCK)
            step, rstep, fstep = blk[:, 0], blk[:, 1], blk[:, 2]
            link(dve.tensor_reduce(step, blocks, AX.X, ALU.max, apply_absolute_value=True))
            link(dve.tensor_scalar(step, step, 1.0 / QMAX_W, MIN_SCALE, ALU.mult, ALU.max))
            link(dve.reciprocal(rstep, step))
            link(dve.tensor_tensor(blocks, blocks, rstep.unsqueeze(2).to_broadcast([P, NBLK, QBLOCK]), ALU.mult))
            link(dve.tensor_scalar(ffn_nat, ffn_nat, ROUNDER, -ROUNDER, ALU.add, ALU.add))
            largest = spread_maxima(3, lambda: dve.tensor_reduce(
                maxima[:, 0:3], step.rearrange("p (w b) -> p w b", w=3), AX.X, ALU.max))
            link(dve.tensor_scalar(TO_F16, largest, QMAX_W, None, ALU.mult))
            link(dve.tensor_scalar(EXP, TO_F16.bitcast(I32), 0x7F800000, None, ALU.bitwise_and))
            link(dve.tensor_scalar(FROM_F16, EXP.bitcast(F32), 2.0**-14, None, ALU.mult))
            link(dve.tensor_scalar(EXP, TO_F16.bitcast(I32), 23, 0xFF, ALU.logical_shift_right, ALU.bitwise_xor))
            link(dve.tensor_scalar(EXP, EXP, 23, None, ALU.logical_shift_left))
            link(dve.tensor_scalar(TO_F16, EXP.bitcast(F32), 2.0**13, None, ALU.mult))
            for w in range(3):
                part = slice(w * NBLK // 3, (w + 1) * NBLK // 3)
                ins = dve.tensor_scalar(fstep[:, part], step[:, part], TO_F16[:, w:w + 1], None, ALU.mult)
            link(ins)
            dve.tensor_tensor(blocks, blocks, fstep.unsqueeze(2).to_broadcast([P, NBLK, QBLOCK]), ALU.mult
                              ).then_inc(ffn_w_quantised, 1)
            for n in range(9):
                dve.wait_ge(ffn_w_hi, n + 1)
                dve.tensor_tensor(w_part(n, 1), w_bank(n), w_part(n, 0), ALU.subtract).then_inc(ffn_w_lo, 1)
            dve.wait_ge(consts_ready, 1)

            def norm_stats(g, c, which, ready, first, second, third):
                hold_on_constant(dve)
                tile_wait(dve, ready, g, c)
                dve.bn_stats(stats6[:, which], h_all[:, at(g * GT + c, 1), :].rearrange("p o d -> p (o d)")
                             ).then_inc(first, 1)
                hold_on_constant(dve)
                tile_wait(dve, first, g, c)
                dve.bn_aggr(meanvar[:, c % 2, which], stats6[:, which]).then_inc(second, 1)
                tile_wait(dve, second, g, c)
                dve.tensor_scalar(vareps[:, c % 2, which:which + 1], meanvar[:, c % 2, which, 1:2], NORM_EPS,
                                  None, ALU.add).then_inc(third, 1)

            def normed(g, c, which, dst, ready, done):
                tile_wait(dve, ready, g, c)
                dve.tensor_scalar(dst[:, c % 2:c % 2 + 1], h_all[:, at(g * GT + c, 1), :],
                                  meanvar[:, c % 2, which, 0:1], rstd[:, c % 2, which:which + 1],
                                  ALU.subtract, ALU.mult).then_inc(done, 1)

            o_bank = lo_bank[:, 0:H * DV].rearrange("p (h d) -> p h d", h=H)

            def iteration(g, u):
                c = u - 3
                if due(g, c):
                    tile_wait(dve, onorm_ready, g, c)
                    dve.tensor_tensor(o_n[:, c % 2].rearrange("p (h d) -> p h d", h=H), o_bank[:, :, 0:DH],
                                      onorm[:, c % 2].unsqueeze(2).to_broadcast([P, H, DH]), ALU.mult
                                      ).then_inc(o_n_ready, 1)
                c = u
                if due(g, c):
                    tile_wait(dve, v_done, g, c)
                    dve.tensor_copy(v_ring[:, c % GT, :, 0:DH],
                                    vws_bank[:, 0:D].rearrange("p (h d) -> p h d", h=H)).then_inc(v_ready, 1)
                c = u + 1
                if due(g, c):
                    slot_wait(dve, gathered[c % GT], g, c, 32)
                    tile_wait(dve, lora_done, g, c)
                    dve.tensor_tensor(h_all[:, at(g * GT + c, 1), :], base_ring[:, c % GT:c % GT + 1, :],
                                      lo_bank[:, 0:D].unsqueeze(1), ALU.add).then_inc(h_ready, 1)
                    norm_stats(g, c, 0, h_ready, stats_done, meanvar_done, vareps_ready)
                c = u - 3
                if due(g, c):
                    tile_wait(dve, attn_done, g, c)
                    dve.tensor_tensor(h_all[:, at(g * GT + c, 1), :], h_all[:, at(g * GT + c, 1), :],
                                      vws_bank[:, 0:D].unsqueeze(1), ALU.add).then_inc(h2_ready, 1)
                    norm_stats(g, c, 1, h2_ready, stats2_done, meanvar2_done, vareps2_ready)
                c = u + 1
                if due(g, c):
                    normed(g, c, 0, xn, rstd_ready, xn_ready)
                c = u - 1
                if due(g, c):
                    tile_wait(dve, scores_done, g, c)
                    for half in range(2):
                        r = slice(2 * half, 2 * half + 2)
                        dve.tensor_tensor(probs[:, c % 2, r].rearrange("p r n t -> p r (n t)"),
                                          scores_ps[:, r, 0:NG * P], causal.rearrange("p (r n) -> p r n", r=2),
                                          ALU.mult).then_inc(probs_ready, 1)
                c = u - 3
                if due(g, c):
                    normed(g, c, 1, xn2, rstd2_ready, xn2_ready)
                c = u - 4
                if due(g, c):
                    hold_on_constant(dve)
                    tile_wait(dve, xn2_t_ready, g, c)
                    dve.tensor_reduce(absmax[:, at(g * GT + c, 1)], xn2_t[:, :, at((g * GT + c) * P, P)],
                                      AX.XY, ALU.max, apply_absolute_value=True).then_inc(absmax_ready, 1)
                c = u - 2
                if due(g, c):
                    tile_wait(dve, squares_ready, g, c)
                    dve.tensor_scalar(denom2[:].unsqueeze(2), squares[:, c % 2, :, DH:DV], 1.0, NORM_EPS,
                                      ALU.max, ALU.mult).then_inc(denom2_done, 1)
                    dve.tensor_reduce(ssq[:], squares[:, c % 2, :, 0:DH], AX.X, ALU.add).then_inc(ssq_done, 1)
                    tile_wait(dve, ssq_done, g, c)
                    tile_wait(dve, denom2_done, g, c)
                    dve.scalar_tensor_tensor(out=meansq[:, c % 2], in0=ssq[:], scalar=1.0 / DH, in1=denom2[:],
                                             op0=ALU.mult, op1=ALU.add).then_inc(meansq_ready, 1)
                    tile_wait(dve, state_done, g, c)
                    dve.tensor_tensor(state_new[:, c % 2], vws_bank[:, 0:NG * SW].rearrange(
                        "p (n w) -> p n w", n=NG), diag, ALU.mult).then_inc(state_masked, 1)

            run_pipeline(dve, iteration)

            dve.wait_ge(absmax_ready, TILES)
            largest = spread_maxima(1, lambda: dve.tensor_reduce(maxima[:, 0:1], absmax[:, 0:TILES], AX.X, ALU.max))
            scale_of(largest, None, S_X, C_X)

            def low_x(n, s):
                dve.wait_ge(xh_ready, n + 1)
                dve.tensor_tensor(xl[:, :, at(n * GW, GW)], x16[:, s], xh[:, :, at(n * GW, GW)], ALU.subtract
                                  ).then_inc(xl_ready, 1)

            low_x(0, 0)
            low_x(1, 1)
            with dve.Fori(1, GROUPS // 2) as q:
                for s in range(2):
                    low_x(q * 2 + s, s)

            def group_max(kept, done):
                def group(n):
                    for k in range(0, MF, 3):
                        hold_on_constant(dve)
                        dve.wait_ge(kept, n * MF + (k + 3))
                        dve.tensor_reduce(absmax[:, at(n * MF + k, 3)],
                                          big[:, at(n * GF + k * GW, 3 * GW)].rearrange("p (m n) -> p m n", m=3),
                                          AX.X, ALU.max, apply_absolute_value=True).then_inc(done, 1)
                return group

            run_groups(dve, group_max(up_kept, up_max), GROUPS)
            dve.wait_ge(up_max, 2 * GROUPS)
            largest = spread_maxima(1, lambda: dve.tensor_reduce(maxima[:, 0:1], absmax[:], AX.X, ALU.max))
            link(dve.tensor_scalar(S_PROD, S_X, FROM_F16[:, 0:1], None, ALU.mult))
            scale_of(largest, S_PROD, S_UP, C_UP)
            dve.wait_ge(scale_ready, 2)

            def quantise_up(n):
                dve.tensor_scalar(quant[:, at(n * GF, GF)], big[:, at(n * GF, GF)], C_UP, None, ALU.mult
                                  ).then_inc(up_quantised, 1)

            gate_group_max = group_max(gate_kept, gate_max)

            def up_and_gate(n):
                quantise_up(n)
                gate_group_max(n)

            run_groups(dve, up_and_gate, GROUPS)
            dve.wait_ge(gate_max, 2 * GROUPS)
            largest = spread_maxima(1, lambda: dve.tensor_reduce(maxima[:, 0:1], absmax[:], AX.X, ALU.max))
            link(dve.tensor_scalar(S_PROD, S_X, FROM_F16[:, 1:2], None, ALU.mult))
            scale_of(largest, S_PROD, S_GATE, C_GATE)
            dve.wait_ge(scale_ready, 3)
            link(dve.tensor_scalar(S_SIG, S_GATE, 1.0 / SIG_STEPS, None, ALU.mult))

            def silu(q):
                for s in range(2):
                    dve.wait_ge(sig_ready, q * 2 + (s + 1))
                    dve.tensor_scalar(sig16[:, s], sig[:, s], SIG_STEPS, QMAX_SIG, ALU.mult, ALU.min
                                      ).then_inc(sig_quantised, 1)
                    dve.wait_ge(sig_quantised, q * 2 + (s + 1))
                    dve.tensor_tensor(big[:, at(q * GF + s * HALF, HALF)], g16[:, s], sig16[:, s], ALU.mult
                                      ).then_inc(silu_ready, 1)
                    hold_on_constant(dve)
                    dve.wait_ge(silu_ready, q * 2 + (s + 1))
                    dve.tensor_reduce(absmax[:, at(q * 2 + s, 1)], big[:, at(q * GF + s * HALF, HALF)], AX.X,
                                      ALU.max, apply_absolute_value=True).then_inc(silu_max, 1)

            run_groups(dve, silu, GROUPS)
            dve.wait_ge(silu_max, 2 * GROUPS)
            largest = spread_maxima(1, lambda: dve.tensor_reduce(
                maxima[:, 0:1], absmax[:, 0:2 * GROUPS], AX.X, ALU.max))
            scale_of(largest, S_SIG, S_SILU, C_SILU)

            def product(q):
                for s in range(2):
                    dve.wait_ge(silu_quantised, q * 2 + (s + 1))
                    dve.tensor_tensor(big[:, at(q * GF + s * HALF, HALF)], g16[:, s],
                                      quant[:, at(q * GF + s * HALF, HALF)], ALU.mult).then_inc(prod_ready, 1)
                    hold_on_constant(dve)
                    dve.wait_ge(prod_ready, q * 2 + (s + 1))
                    dve.tensor_reduce(absmax[:, at(q * 2 + s, 1)], big[:, at(q * GF + s * HALF, HALF)], AX.X,
                                      ALU.max, apply_absolute_value=True).then_inc(prod_max, 1)

            run_groups(dve, product, GROUPS)
            dve.wait_ge(prod_max, 2 * GROUPS)
            largest = spread_maxima(1, lambda: dve.tensor_reduce(
                maxima[:, 0:1], absmax[:, 0:2 * GROUPS], AX.X, ALU.max))
            dve.wait_ge(scale_ready, 4)
            link(dve.tensor_scalar(T1, S_SILU, S_UP, None, ALU.mult))
            link(dve.tensor_copy(S_SIG, T1))
            scale_of(largest, S_SIG, S_PROD, C_PROD)
            dve.wait_ge(scale_ready, 5)
            link(dve.tensor_scalar(S_OUT, S_PROD, FROM_F16[:, 2:3], None, ALU.mult))

            def finish(q):
                for s in range(2):
                    dve.wait_ge(oh_ready, q * 2 + (s + 1))
                    dve.tensor_tensor(ol[:, s], o16[:].rearrange("p (m n) -> p m n", m=MF), oh[:, s],
                                      ALU.subtract).then_inc(ol_ready, 1)
                for s in range(2):
                    slot = res_loaded[s]
                    dve.wait_ge(slot, q * 16 + 16)
                    for t in range(GT):
                        dve.wait_ge(down_done, q * (2 * GT) + (s * GT + t + 1))
                        dve.scalar_tensor_tensor(out=res[:, s, t], in0=banks[(s * GT + t) % 8][:, 0:D],
                                                 scalar=S_OUT, in1=res[:, s, t], op0=ALU.mult, op1=ALU.add
                                                 ).then_inc(out_ready, 1)

            run_groups(dve, finish, GROUPS // 2)

        @block.tensor
        def _(pe):
            barriers = [0]

            def spread_maxima(n):
                barriers[0] += 1
                pe.wait_ge(maxima_ready, barriers[0])
                pe.transpose(turn_bank[0:n, 0:P], maxima[:, 0:n], ident[:]).then_inc(maxima_turned, 1)
                pe.wait_ge(pick_ready, barriers[0])
                pe.matmul(turn_bank[:, 0:n], ones[0:n, :], pick[0:n, 0:n], start=True, stop=True
                          ).then_inc(top_spread, 1)

            pe.wait_ge(ident_ready, 1)
            pe.wait_ge(idx_rows_ready, 1)
            pe.transpose(turn_bank[:, 0:TILES], idx_rows, ident[0:TILES, 0:TILES]).then_inc(idx_turned, 1)
            pe.wait_ge(attn_w_loaded, 16 * (1 + 4 + HG))
            for n in range(4):
                for k in range(KD):
                    for o in range(OT):
                        last = pe.transpose(banks[n][:, k * D + o * P:k * D + (o + 1) * P],
                                            attn_nat[:, n, o, k * P:(k + 1) * P], ident[:])
                last.then_inc(attn_w_turned, 1)
            pe.wait_ge(consts_ready, 1)
            spread_maxima(3)
            pe.wait_ge(ffn_w_quantised, 1)
            for n in range(9):
                if n >= 3:
                    if n < 6:
                        pe.wait_ge(qkv_w_ready, n - 2)
                    elif n == 6:
                        pe.wait_ge(wo_ready, 1)
                    else:
                        pe.wait_ge(ffn_w_lo, n - 6)
                which, k0 = n // 3, 2 * (n % 3)
                nat = ffn_nat[:, which * KD * FF:(which + 1) * KD * FF]
                for a in range(2):
                    for b in range(2):
                        if which < 2:
                            src = nat.rearrange("p (o n) -> p o n", n=D)[:, k0 + b, a * P:(a + 1) * P]
                        else:
                            src = nat.rearrange("p (o n) -> p o n", n=FF)[:, b, (k0 + a) * P:(k0 + a + 1) * P]
                        last = pe.transpose(w_bank(n)[:, a, b * P:(b + 1) * P], src, ident[:])
                last.then_inc(ffn_w_turned, 1)
            pe.wait_ge(ffn_w_lo, 9)
            pe.wait_ge(lora_b_ready, 1)
            pe.wait_ge(qkv_w_ready, 3)
            pe.wait_ge(wo_ready, 1)
            pe.wait_ge(idx_ready, 1)

            def free_turn_bank(g, u):
                tile_wait(pe, xn2_t_ready, g, u - 4)
                if fixed(g):
                    tile_wait(pe, o_t_ready, g, u - 3)
                    tile_wait(pe, lora_t_ready, g, u + 1)
                    tile_wait(pe, xn_t_ready, g, u)

            def iteration(g, u):
                c = u
                if due(g, c):
                    tile_wait(pe, xn_t_ready, g, c)
                    tile_wait(pe, qkt_ready, g, c - 1)
                    for k in range(KD):
                        last = pe.matmul(qk_bank[:], xn_t[:, c % 2, k], wqkv_t[:, k, 0:2 * D],
                                         start=(k == 0), stop=(k == KD - 1))
                    last.then_inc(qk_done, 1)
                    tile_wait(pe, state_masked, g, c - 3)
                    for k in range(KD):
                        last = pe.matmul(vws_bank[:, 0:D], xn_t[:, c % 2, k], wqkv_t[:, k, 2 * D:3 * D],
                                         start=(k == 0), stop=(k == KD - 1))
                    last.then_inc(v_done, 1)
                c = u - 3
                if due(g, c):
                    tile_wait(pe, o_n_ready, g, c)
                    tile_wait(pe, xn_t_ready, g, u)
                    tile_wait(pe, lora_t_ready, g, u + 1)
                    if fixed(g):
                        tile_wait(pe, xn2_t_ready, g, u - 5)
                    for k in range(KD):
                        last = pe.transpose(turn_bank[:, k * P:(k + 1) * P], o_n[:, c % 2, k * P:(k + 1) * P],
                                            ident[:])
                    last.then_inc(o_turned, 1)
                c = u + 1
                if due(g, c):
                    tile_wait(pe, lora_t_ready, g, c)
                    pe.matmul(lo_bank[:, 0:D], lora_t[0:R, c % 2], lora_b2[0:R, :], start=True, stop=True
                              ).then_inc(lora_done, 1)
                c = u - 3
                if due(g, c):
                    tile_wait(pe, o_t_ready, g, c)
                    tile_wait(pe, v_ready, g, u)
                    if fixed(g):
                        tile_wait(pe, state_masked, g, c)
                    for k in range(KD):
                        last = pe.matmul(vws_bank[:, 0:D], o_t[:, c % 2, k], wo_t[:, k], start=(k == 0),
                                         stop=(k == KD - 1))
                    last.then_inc(attn_done, 1)
                c = u - 1
                if due(g, c):
                    tile_wait(pe, qkt_ready, g, c)
                    tile_wait(pe, probs_ready, g, c - 1, 2)
                    for n in range(NG):
                        for r in range(HG):
                            rows = slice(r * DH, (r + 1) * DH)
                            last = pe.matmul(scores_ps[:, r, n * P:(n + 1) * P], qkt_ring[rows, c % GT, NG + n],
                                             qkt_ring[rows, c % GT, n], start=True, stop=True)
                    last.then_inc(scores_done, 1)
                c = u
                if due(g, c):
                    tile_wait(pe, qk_ready, g, c)
                    for n in range(2 * NG):
                        last = pe.transpose(qk_bank[:, n * P:(n + 1) * P], qk_ring[:, c % GT, n * P:(n + 1) * P],
                                            ident[:])
                    last.then_inc(qk_turned, 1)
                c = u - 4
                if due(g, c):
                    tile_wait(pe, xn2_ready, g, c)
                    tile_wait(pe, o_t_ready, g, u - 3)
                    if fixed(g):
                        tile_wait(pe, xn2_t_ready, g, u - 5)
                    for k in range(KD):
                        last = pe.transpose(turn_bank[:, k * P:(k + 1) * P], xn2[:, c % 2, k * P:(k + 1) * P],
                                            ident[:])
                    last.then_inc(xn2_turned, 1)
                c = u - 2
                if due(g, c):
                    tile_wait(pe, state_ready, g, u - 4)
                    tile_wait(pe, h_ready, g, u + 1)
                    if fixed(g):
                        tile_wait(pe, o_n_ready, g, u - 3)
                    for n in range(NG):
                        pe.matmul(lo_bank[:, n * SW:(n + 1) * SW], qkt_ring[:, c % GT, n], state[:, c % B, n],
                                  start=(n == 0), stop=False, skip_group_check=True)
                    tile_wait(pe, probs_ready, g, c, 2)
                    tile_wait(pe, v_ready, g, c)
                    for h in range(H):
                        last = pe.matmul(lo_bank[:, h * DV:(h + 1) * DV], probs[:, c % 2, h % HG, h // HG],
                                         v_ring[:, c % GT, h], start=False, stop=(h == H - 1),
                                         skip_group_check=True)
                    last.then_inc(o_done, 1)
                    tile_wait(pe, h2_ready, g, u - 3)
                    if fixed(g):
                        tile_wait(pe, v_ready, g, u)
                    for n in range(NG):
                        last = pe.matmul(vws_bank[:, n * SW:(n + 1) * SW],
                                         qk_ring[:, c % GT, D + n * P:D + (n + 1) * P],
                                         v_ring[:, c % GT, n * HG:(n + 1) * HG].rearrange("p h d -> p (h d)"),
                                         start=(n == 0), stop=(n == NG - 1), skip_group_check=True)
                    last.then_inc(state_done, 1)
                c = u + 2
                if due(g, c):
                    hold_on_constant(pe)
                    slot_wait(pe, gathered[c % GT], g, c, 32)
                    free_turn_bank(g, u)
                    pe.transpose(turn_bank[0:R, KD * P:KD * P + P], lora_ring[:, c % GT], ident[:]
                                 ).then_inc(lora_turned, 1)
                c = u + 1
                if due(g, c):
                    tile_wait(pe, xn_ready, g, c)
                    free_turn_bank(g, u)
                    for k in range(KD):
                        last = pe.transpose(turn_bank[:, k * P:(k + 1) * P], xn[:, c % 2, k * P:(k + 1) * P],
                                            ident[:])
                    last.then_inc(xn_turned, 1)

            run_pipeline(pe, iteration)

            def project(n, m, hi, lo, done):
                for k in range(KD):
                    cols = slice(m * P, (m + 1) * P)
                    xs = at(n * GW, GW)
                    pe.matmul(banks[m], hi[:, k, cols], xh[:, k, xs], start=(k == 0), stop=False)
                    pe.matmul(banks[m], hi[:, k, cols], xl[:, k, xs], start=False, stop=False)
                    last = pe.matmul(banks[m], lo[:, k, cols], xh[:, k, xs], start=False, stop=(k == KD - 1))
                last.then_inc(done, 1)

            spread_maxima(1)
            pe.wait_ge(xn2_t_ready, TILES)

            def up_group(n):
                pe.wait_ge(xl_ready, n + 1)
                for m in range(MF):
                    if not fixed(n) or n >= 1:
                        pe.wait_ge(up_kept, n * MF + (m + 1 - MF))
                    project(n, m, up_hi, up_lo, up_done)

            run_groups(pe, up_group, GROUPS)

            def gate_group(n):
                for m in range(MF):
                    if fixed(n) and n == 0:
                        pe.wait_ge(up_kept, (GROUPS - 1) * MF + m + 1)
                    else:
                        pe.wait_ge(gate_kept, n * MF + (m + 1 - MF))
                    project(n, m, gate_hi, gate_lo, gate_done)
                    if fixed(n) and m == 1:
                        spread_maxima(1)

            run_groups(pe, gate_group, GROUPS)
            for _ in range(3):
                spread_maxima(1)
            pe.wait_ge(gate_kept, GROUPS * MF)
            pe.wait_ge(scale_ready, 5)

            def down_pair(q):
                for s in range(2):
                    pe.wait_ge(ol_ready, q * 2 + (s + 1))
                    for t in range(GT):
                        bank = banks[(s * GT + t) % 8]
                        if not fixed(q) or q >= 1:
                            pe.wait_ge(out_ready, q * (2 * GT) + (s * GT + t + 1 - 2 * GT))
                        ts = slice(t * P, (t + 1) * P)
                        for m in range(MF):
                            pe.matmul(bank[:, 0:D], oh[:, s, m, ts], down_hi[:, m], start=(m == 0), stop=False)
                            pe.matmul(bank[:, 0:D], oh[:, s, m, ts], down_lo[:, m], start=False, stop=False)
                            last = pe.matmul(bank[:, 0:D], ol[:, s, m, ts], down_hi[:, m], start=False,
                                             stop=(m == MF - 1))
                        last.then_inc(down_done, 1)

            run_groups(pe, down_pair, GROUPS // 2)


_INS = ["x", "L0_tok_base_weight", "L0_tok_lora_A", "L0_tok_lora_B", "L0_attn_Wq", "L0_attn_Wk", "L0_attn_Wv",
        "L0_attn_Wo", "L0_attn_norm_w", "L0_ffn_w_gate", "L0_ffn_w_up", "L0_ffn_w_down"]


def kernel(**inputs):
    import numpy as _np
    import concourse.bacc as _bacc
    from concourse import mybir as _mybir
    from concourse.bass_utils import run_bass_kernel_spmd as _run

    nc = _bacc.Bacc("TRN2", target_bir_lowering=False, num_devices=1)
    arrays, args = {}, []
    for name in _INS:
        a = _np.ascontiguousarray(inputs[name])
        arrays[f"in_{name}"] = a
        args.append(nc.dram_tensor(f"in_{name}", a.shape, _mybir.dt.from_np(a.dtype), kind="ExternalInput").ap())
    batch, length = inputs["x"].shape
    width = inputs["L0_tok_base_weight"].shape[1]
    args.append(nc.dram_tensor("out_h", (batch, length, width), _mybir.dt.float32, kind="ExternalOutput").ap())
    lm_tower(nc, *args)
    r = _run(nc, [arrays], core_ids=[0])
    return r.results[0]["out_h"]
```

```python
from contextlib import ExitStack

import concourse.bass as bass
from concourse import mybir

ALU = mybir.AluOpType
ACT = mybir.ActivationFunctionType
AX = mybir.AxisListType
F32 = mybir.dt.float32
F16 = mybir.dt.float16
I16 = mybir.dt.int16
U16 = mybir.dt.uint16
I32 = mybir.dt.int32

P = 128
NORM_EPS = 1e-5
LORA_SCALING = 2.0
QMAX_ACT = 2.0**15 - 1.0
QMAX_W = 2.0**3 - 1.0
QMAX_SIG = 65535.0
SIG_STEPS = 65536.0
MIN_SCALE = 1e-12
QBLOCK = 32
ROUNDER = 12582912.0


def lm_tower(nc, x, base, lora_a, lora_b, wq, wk, wv, wo, norm_w, w_gate, w_up, w_down, out):
    B, S = x.shape
    D = base.shape[1]
    R = lora_a.shape[1]
    DH = norm_w.shape[0]
    H = D // DH
    FF = w_gate.shape[0]
    TILES = B * S // P
    CHUNKS = S // P
    KD = D // P
    MF = FF // P
    HG = P // DH
    NG = H // HG
    DV = DH + 1
    SW = HG * DV
    GT = 4
    GW = GT * P
    GROUPS = TILES // GT
    GF = MF * GW
    HALF = GF // 2
    OT = D // P
    SLOTS = 4
    HALVES = 2 * GROUPS
    assert B == 2 and KD == 2 and NG == 2 and MF % 3 == 0 and TILES % GT == 0 and R <= 32

    h2_dram = nc.dram_tensor("h2_kept", (TILES, P, D), F32, kind="Internal").ap()

    with ExitStack() as ctx:
        def sb(name, shape, dt=F32):
            return ctx.enter_context(nc.sbuf_tensor(name, shape, dt))

        def sem(name):
            return ctx.enter_context(nc.semaphore(name))

        big = sb("big", [P, GROUPS * GF])
        quant = sb("quant", [P, GROUPS * GF], I16)
        xregion = sb("xregion", [P, 2 * KD * TILES * P], F16)
        ident = sb("ident", [P, P])
        ones = sb("ones", [P, P])
        minus_half = sb("minus_half", [P, H])
        up_hi = sb("up_hi", [P, KD, FF], F16)
        up_lo = sb("up_lo", [P, KD, FF], F16)
        gate_hi = sb("gate_hi", [P, KD, FF], F16)
        gate_lo = sb("gate_lo", [P, KD, FF], F16)
        down_hi = sb("down_hi", [P, MF, D], F16)
        down_lo = sb("down_lo", [P, MF, D], F16)
        absmax = sb("absmax", [P, GROUPS * MF])
        maxima = sb("maxima", [P, 4])
        top = sb("top", [P, 4])
        pick = sb("pick", [P, 4])
        scales = sb("scales", [P, 32])
        idx = sb("idx", [P, TILES], I32)
        table_loader = sb("table_loader", [P, 1])
        idx_slot = sb("idx_slot", [P, GT], I32)
        stats6 = sb("stats6", [P, 2, 6])
        meanvar = sb("meanvar", [P, 2, 2, 2])
        vareps = sb("vareps", [P, 2, 2])
        rstd = sb("rstd", [P, 2, 2])
        ssq = sb("ssq", [P, H])
        denom2 = sb("denom2", [P, H])
        meansq = sb("meansq", [P, 2, H])
        onorm = sb("onorm", [P, 2, H])

        big_at = [0]

        def in_big(shape):
            n = 1
            for k in shape:
                n *= k
            v = big[:, big_at[0]:big_at[0] + n]
            big_at[0] += n
            assert big_at[0] <= GROUPS * GF
            names = "abcd"[:len(shape)]
            if len(shape) == 1:
                return v
            return v.rearrange(f"p ({' '.join(names)}) -> p {' '.join(names)}",
                               **{c: k for c, k in zip(names[1:], shape[1:])})

        h_all = in_big([TILES, D])
        base_ring = in_big([GT, D])
        lora_ring = in_big([GT, R])
        lora_t = in_big([2, P])
        xn = in_big([2, D])
        xn_t = in_big([2, KD, P])
        qk_ring = in_big([GT, 2 * D])
        v_ring = in_big([GT, H, DV])
        qkt_ring = in_big([GT, 2 * NG, P])
        probs = in_big([2, HG, NG, P])
        state = in_big([B, NG, SW])
        state_new = in_big([2, NG, SW])
        diag = in_big([NG, SW])
        squares = in_big([2, H, DV])
        o_n = in_big([2, D])
        o_t = in_big([2, KD, P])
        xn2 = in_big([2, D])

        xreg32 = xregion[:].bitcast(F32)
        x_at = [0]

        def in_x(n):
            v = xreg32[:, x_at[0]:x_at[0] + n]
            x_at[0] += n
            assert x_at[0] <= KD * TILES * P
            return v

        wqkv_t = in_x(KD * 3 * D).rearrange("p (k n) -> p k n", k=KD)
        wo_t = in_x(KD * D).rearrange("p (k n) -> p k n", k=KD)
        lora_b2 = in_x(D)
        causal = in_x(2 * NG * P)
        norm_col = in_x(1)
        ffn_nat = in_x(3 * KD * FF)
        quant32 = quant[:].bitcast(F32)
        xn2_t = quant32[:, 0:KD * TILES * P].rearrange("p (k n) -> p k n", k=KD)
        attn_nat = quant32[:, KD * TILES * P:KD * TILES * P + 4 * KD * D].rearrange(
            "p (w k n) -> p w k n", w=4, k=KD)
        x16 = quant[:, 2 * KD * TILES * P:2 * KD * TILES * P + 2 * KD * GW].rearrange(
            "p (s k n) -> p s k n", s=2, k=KD)
        NBLK = 3 * KD * FF // QBLOCK
        blk = big[:, big_at[0]:big_at[0] + 3 * NBLK].rearrange("p (a b) -> p a b", a=3)
        idx_rows = big[0:TILES, big_at[0] + 3 * NBLK:big_at[0] + 3 * NBLK + P]
        idx_raw = big[0:TILES, big_at[0] + 3 * NBLK + P:big_at[0] + 3 * NBLK + 2 * P].bitcast(I32)

        xh = xregion[:, 0:KD * TILES * P].rearrange("p (k n) -> p k n", k=KD)
        xl = xregion[:, KD * TILES * P:2 * KD * TILES * P].rearrange("p (k n) -> p k n", k=KD)
        assert KD * FF == HALF
        g16 = [w[:].rearrange("p k n -> p (k n)").bitcast(I16) for w in (up_hi, up_lo, gate_hi, gate_lo)]
        sig = xregion[:, 0:8 * HALF].bitcast(F32).rearrange("p (s n) -> p s n", s=SLOTS)
        sig_steps = xregion[:, 0:8 * HALF].bitcast(I32).rearrange("p (s n) -> p s n", s=SLOTS)
        sig16 = xregion[:, 8 * HALF:10 * HALF].bitcast(U16).rearrange("p (s n) -> p s n", s=2)
        oh = xregion[:, 0:2 * GF].rearrange("p (s m n) -> p s m n", s=2, m=MF)
        ol = xregion[:, 2 * GF:4 * GF].rearrange("p (s m n) -> p s m n", s=2, m=MF)
        res = xregion[:, 4 * GF:4 * GF + 4 * GT * D].bitcast(F32).rearrange(
            "p (s t d) -> p s t d", s=2, t=GT)
        o16 = quant[:, 0:2 * GF].rearrange("p (s m n) -> p s m n", s=2, m=MF)

        scores_ps = ctx.enter_context(nc.psum_tensor("scores_ps", [P, HG, 512], F32))
        qk_bank = ctx.enter_context(nc.psum_tensor("qk_bank", [P, 512], F32))
        vws_bank = ctx.enter_context(nc.psum_tensor("vws_bank", [P, 512], F32))
        lo_bank = ctx.enter_context(nc.psum_tensor("lo_bank", [P, 512], F32))
        turn_bank = ctx.enter_context(nc.psum_tensor("turn_bank", [P, 512], F32))
        banks = [scores_ps[:, n, :] for n in range(HG)] + [qk_bank[:], vws_bank[:], lo_bank[:], turn_bank[:]]

        x_loaded = sem("x_loaded")
        attn_w_loaded = sem("attn_w_loaded")
        ffn_w_loaded = sem("ffn_w_loaded")
        ident_ready = sem("ident_ready")
        consts_ready = sem("consts_ready")
        pool_chain = sem("pool_chain")
        idx_rows_ready = sem("idx_rows_ready")
        idx_turned = sem("idx_turned")
        idx_ready = sem("idx_ready")
        lora_b_ready = sem("lora_b_ready")
        attn_w_turned = sem("attn_w_turned")
        qkv_w_ready = sem("qkv_w_ready")
        wo_ready = sem("wo_ready")
        ffn_w_quantised = sem("ffn_w_quantised")
        ffn_w_turned = sem("ffn_w_turned")
        ffn_w_hi = sem("ffn_w_hi")
        ffn_w_lo = sem("ffn_w_lo")
        ffn_scales_ready = sem("ffn_scales_ready")
        steps_ready = sem("steps_ready")
        dve_chain = sem("dve_chain")
        maxima_ready = sem("maxima_ready")
        maxima_turned = sem("maxima_turned")
        pick_ready = sem("pick_ready")
        top_spread = sem("top_spread")
        scale_ready = sem("scale_ready")
        slot_ready = sem("slot_ready")
        gathered = [sem(f"gathered{n}") for n in range(GT)]
        lora_turned = sem("lora_turned")
        lora_t_ready = sem("lora_t_ready")
        lora_done = sem("lora_done")
        h_ready = sem("h_ready")
        stats_done = sem("stats_done")
        meanvar_done = sem("meanvar_done")
        vareps_ready = sem("vareps_ready")
        rstd_ready = sem("rstd_ready")
        xn_ready = sem("xn_ready")
        xn_turned = sem("xn_turned")
        xn_t_ready = sem("xn_t_ready")
        qk_done = sem("qk_done")
        qk_ready = sem("qk_ready")
        v_done = sem("v_done")
        v_ready = sem("v_ready")
        qk_turned = sem("qk_turned")
        qkt_ready = sem("qkt_ready")
        scores_done = sem("scores_done")
        probs_ready = sem("probs_ready")
        o_done = sem("o_done")
        squares_ready = sem("squares_ready")
        ssq_done = sem("ssq_done")
        denom2_done = sem("denom2_done")
        meansq_ready = sem("meansq_ready")
        onorm_ready = sem("onorm_ready")
        o_n_ready = sem("o_n_ready")
        o_turned = sem("o_turned")
        o_t_ready = sem("o_t_ready")
        state_done = sem("state_done")
        state_masked = sem("state_masked")
        state_ready = sem("state_ready")
        attn_done = sem("attn_done")
        h2_ready = sem("h2_ready")
        h2_stored = [sem(f"h2_stored{n}") for n in range(GT)]
        stats2_done = sem("stats2_done")
        meanvar2_done = sem("meanvar2_done")
        vareps2_ready = sem("vareps2_ready")
        rstd2_ready = sem("rstd2_ready")
        xn2_ready = sem("xn2_ready")
        xn2_turned = sem("xn2_turned")
        xn2_t_ready = sem("xn2_t_ready")
        absmax_ready = sem("absmax_ready")
        x16_ready = sem("x16_ready")
        xh_ready = sem("xh_ready")
        xl_ready = sem("xl_ready")
        up_done = sem("up_done")
        up_kept = sem("up_kept")
        up_max = sem("up_max")
        up_quantised = sem("up_quantised")
        gate_done = sem("gate_done")
        gate_kept = sem("gate_kept")
        gate_max = sem("gate_max")
        gate_quantised = sem("gate_quantised")
        sig_ready = sem("sig_ready")
        sig_quantised = sem("sig_quantised")
        silu_ready = sem("silu_ready")
        silu_max = sem("silu_max")
        silu_quantised = sem("silu_quantised")
        prod_ready = sem("prod_ready")
        prod_max = sem("prod_max")
        o16_ready = sem("o16_ready")
        oh_ready = sem("oh_ready")
        ol_ready = sem("ol_ready")
        down_done = sem("down_done")
        res_loaded = [sem(f"res_loaded{n}") for n in range(2)]
        out_ready = sem("out_ready")
        out_stored = [sem(f"out_stored{n}") for n in range(2)]

        def fixed(n):
            return isinstance(n, int)

        def at(start, n):
            return slice(start, start + n) if fixed(start) else bass.ds(start, n)

        def due(g, c):
            return not fixed(g) or 0 <= GT * g + c < TILES

        def tile_wait(eng, s, g, c, per=1):
            if not fixed(g):
                eng.wait_ge(s, g * (GT * per) + (c + 1) * per)
            elif GT * g + c >= 0:
                eng.wait_ge(s, min(GT * g + c + 1, TILES) * per)

        def slot_wait(eng, s, g, c, per):
            eng.wait_ge(s, g * per + (c // GT + 1) * per)

        def hold_on_constant(eng):
            eng.wait_ge(consts_ready, 1)

        def run_pipeline(eng, iteration):
            for i in range(-2, GT):
                iteration(i // GT, i % GT)
            with eng.Fori(1, TILES // GT - 1) as g:
                for u in range(GT):
                    iteration(g, u)
            for i in range(TILES - GT, TILES + 4):
                iteration(i // GT, i % GT)

        def half_due(q, c):
            return not fixed(q) or 0 <= SLOTS * q + c < HALVES

        def half_wait(eng, s, q, c):
            if not fixed(q) or SLOTS * q + c >= 0:
                eng.wait_ge(s, q * SLOTS + (c + 1))

        def steps_on_act(q, c):
            return c % 2 == 1 and half_due(q, c) and not (fixed(q) and SLOTS * q + c == HALVES - 1)

        def run_halves(eng, half):
            for c in range(-1, SLOTS):
                half(0, c)
            with eng.Fori(1, HALVES // SLOTS - 1) as q:
                for c in range(SLOTS):
                    half(q, c)
            for c in range(SLOTS + 1):
                half(HALVES // SLOTS - 1, c)

        def run_groups(eng, group, n):
            group(0)
            with eng.Fori(1, n) as k:
                group(k)

        def w_part(n, low):
            which, k = n // 3, 2 * (n % 3)
            if which == 2:
                return (down_hi, down_lo)[low][:, k:k + 2, :]
            return ((up_hi, up_lo), (gate_hi, gate_lo))[which][low][:, :, k * P:(k + 2) * P]

        def w_bank(n):
            return banks[n % HG].rearrange("p (k n) -> p k n", k=2)

        def weights_due(g, u):
            if not fixed(g) or GT * g + u <= TILES:
                return range(0)
            first = HG * (GT * g + u - TILES - 1)
            return range(first, min(first + HG, 9))

        block = ctx.enter_context(nc.Block())

        (S_X, C_X, S_UP, C_UP, S_GATE, C_GATE, S_SILU, C_SILU, S_PROD, C_PROD, S_OUT, S_SIG,
         T0, T1) = (scales[:, n:n + 1] for n in range(14))
        EXP = scales[:, 14:17].bitcast(I32)
        TO_F16 = scales[:, 17:20]
        FROM_F16 = scales[:, 20:23]

        @block.sync
        def _(sp):
            sp.dma_start(idx_raw, x.rearrange("b (c p) -> (b c) p", p=P)).then_inc(x_loaded, 16)
            sp.dma_start(lora_b2[0:R, :], lora_b).then_inc(attn_w_loaded, 16)
            for n, w in enumerate((wq, wk, wv, wo)):
                sp.dma_start(attn_nat[:, n], w.rearrange("(k p) n -> p k n", p=P)).then_inc(attn_w_loaded, 16)
            for r in range(HG):
                sp.dma_start(norm_col[r * DH:(r + 1) * DH, :],
                             norm_w.rearrange("(d o) -> d o", o=1)).then_inc(attn_w_loaded, 16)
            for n, w in enumerate((w_up, w_gate, w_down)):
                width = KD * FF
                sp.dma_start(ffn_nat[:, n * width:(n + 1) * width].rearrange("p (k n) -> p k n", n=w.shape[1]),
                             w.rearrange("(k p) n -> p k n", p=P)).then_inc(ffn_w_loaded, 16)

            def iteration(g, u):
                c = u - 3
                if due(g, c):
                    tile_wait(sp, h2_ready, g, c)
                    sp.dma_start(h2_dram[at(g * GT + c, 1)].rearrange("o p d -> p (o d)"),
                                 h_all[:, at(g * GT + c, 1), :].rearrange("p o d -> p (o d)")
                                 ).then_inc(h2_stored[c % GT], 16)

            run_pipeline(sp, iteration)
            for n in range(GT):
                sp.wait_ge(h2_stored[n], 16 * (TILES // GT))

            out_v = out.rearrange("b (c p) d -> b p c d", p=P)

            def load(pair, s):
                sp.dma_start(res[:, s], h2_dram[at(pair * 2 * GT + s * GT, GT)].rearrange("t p d -> p t d")
                             ).then_inc(res_loaded[s], 16)

            def store(pair, s):
                for b in range(B):
                    sp.dma_start(out_v[b, :, at(pair * 4 + s * 2, 2), :],
                                 res[:, s].rearrange("p (c b) d -> p b c d", b=B)[:, b]
                                 ).then_inc(out_stored[s], 16)

            sp.wait_ge(prod_max, 2 * GROUPS)
            load(0, 0)
            load(0, 1)

            def pair_of_groups(q):
                for s in range(2):
                    sp.wait_ge(out_ready, q * (2 * GT) + (s + 1) * GT)
                    store(q, s)
                for s in range(2):
                    sp.wait_ge(out_stored[s], q * 32 + 32)
                    load(q + 1, s)

            with sp.Fori(0, GROUPS // 2 - 1) as q:
                pair_of_groups(q)
            last = GROUPS // 2 - 1
            for s in range(2):
                sp.wait_ge(out_ready, last * 2 * GT + (s + 1) * GT)
                store(last, s)
            for s in range(2):
                sp.wait_ge(out_stored[s], 32 * (GROUPS // 2))

        @block.gpsimd
        def _(pool):
            chain = [0]

            def link(ins):
                chain[0] += 1
                ins.then_inc(pool_chain, 1)
                pool.wait_ge(pool_chain, chain[0])

            link(pool.memset(ident[:], 0.0))
            pool.affine_select(out=ident[:], in_=ident[:], compare_op=ALU.not_equal, fill=1.0, base=0,
                               pattern=[[-1, P]], channel_multiplier=1).then_inc(ident_ready, 1)
            link(pool.memset(ones[:], 1.0))
            link(pool.memset(minus_half[:], -0.5))
            link(pool.memset(causal, 1.0))
            link(pool.affine_select(out=causal.rearrange("p (n t) -> p n t", t=P),
                                    in_=causal.rearrange("p (n t) -> p n t", t=P),
                                    compare_op=ALU.is_ge, fill=0.0, base=0, pattern=[[0, 2 * NG], [1, P]],
                                    channel_multiplier=-1))
            link(pool.memset(diag, 0.0))
            for r in range(HG):
                link(pool.memset(diag[r * DH:(r + 1) * DH, :, r * DV:(r + 1) * DV], 1.0))
            link(pool.memset(state, 0.0))
            pool.memset(v_ring, 1.0).then_inc(consts_ready, 1)

            def gather(n):
                for dst, table in ((base_ring, base), (lora_ring, lora_a)):
                    pool.indirect_dma_start(
                        dst[:, n], None, table,
                        bass.IndirectOffsetOnAxis(ap=idx_slot[:, n:n + 1], axis=0)).then_inc(gathered[n], 16)

            pool.wait_ge(idx_ready, 1)
            pool.tensor_copy(idx_slot[:], idx[:, 0:GT]).then_inc(slot_ready, GT)
            pool.wait_ge(slot_ready, GT)
            for n in range(GT):
                gather(n)

            def iteration(g, u):
                fetch = due(g, u) and due(g, u + GT)
                if fetch:
                    hold_on_constant(pool)
                    tile_wait(pool, h_ready, g, u)
                    tile_wait(pool, lora_turned, g, u)
                    pool.tensor_copy(idx_slot[:, u:u + 1], idx[:, at(g * GT + u + GT, 1)]).then_inc(slot_ready, 1)
                c = u + 1
                if due(g, c):
                    tile_wait(pool, vareps_ready, g, c)
                    if fetch:
                        tile_wait(pool, slot_ready, g, u + GT)
                    pool.tensor_tensor(rstd[:, c % 2, 0:1], vareps[:, c % 2, 0:1], minus_half[:, 0:1],
                                       ALU.pow).then_inc(rstd_ready, 1)
                if fetch:
                    gather(u)
                c = u - 3
                if due(g, c):
                    tile_wait(pool, vareps2_ready, g, c)
                    pool.tensor_tensor(rstd[:, c % 2, 1:2], vareps[:, c % 2, 1:2], minus_half[:, 0:1],
                                       ALU.pow).then_inc(rstd2_ready, 1)
                c = u - 2
                if due(g, c):
                    tile_wait(pool, meansq_ready, g, c)
                    pool.tensor_tensor(onorm[:, c % 2], meansq[:, c % 2], minus_half[:], ALU.pow
                                       ).then_inc(onorm_ready, 1)
                    tile_wait(pool, state_masked, g, c)
                    pool.tensor_tensor(state[:, c % B], state[:, c % B], state_new[:, c % 2], ALU.add
                                       ).then_inc(state_ready, 1)

            run_pipeline(pool, iteration)

        @block.scalar
        def _(act):
            def copy(dst, src, scale=1.0):
                return act.activation(dst, src, ACT.Copy, scale=scale)

            for n in range(3):
                act.wait_ge(attn_w_turned, n + 1)
                copy(wqkv_t[:, :, n * D:(n + 1) * D], banks[n].rearrange("p (k n) -> p k n", k=KD)
                     ).then_inc(qkv_w_ready, 1)
            act.wait_ge(consts_ready, 1)

            def iteration(g, u):
                c = u
                if due(g, c):
                    tile_wait(act, qk_done, g, c)
                    copy(qk_ring[:, c % GT], qk_bank[:]).then_inc(qk_ready, 1)
                c = u - 3
                if due(g, c):
                    tile_wait(act, o_turned, g, c)
                    copy(o_t[:, c % 2], turn_bank[:, 0:KD * P].rearrange("p (k n) -> p k n", k=KD)
                         ).then_inc(o_t_ready, 1)
                c = u - 4
                if due(g, c):
                    hold_on_constant(act)
                    tile_wait(act, xn2_turned, g, c)
                    copy(xn2_t[:, :, at((g * GT + c) * P, P)],
                         turn_bank[:, KD * P:2 * KD * P].rearrange("p (k n) -> p k n", k=KD)
                         ).then_inc(xn2_t_ready, 1)
                c = u
                if due(g, c):
                    tile_wait(act, qk_turned, g, c)
                    copy(qkt_ring[:, c % GT], qk_bank[:].rearrange("p (k n) -> p k n", k=2 * NG)
                         ).then_inc(qkt_ready, 1)
                c = u + 1
                if due(g, c):
                    tile_wait(act, xn_turned, g, c)
                    copy(xn_t[:, c % 2], turn_bank[:, 0:KD * P].rearrange("p (k n) -> p k n", k=KD)
                         ).then_inc(xn_t_ready, 1)
                c = u + 2
                if due(g, c):
                    tile_wait(act, lora_turned, g, c)
                    copy(lora_t[0:R, c % 2], turn_bank[0:R, KD * P:KD * P + P]).then_inc(lora_t_ready, 1)
                c = u - 2
                if due(g, c):
                    tile_wait(act, o_done, g, c)
                    act.activation(squares[:, c % 2], lo_bank[:, 0:H * DV].rearrange(
                        "p (h d) -> p h d", h=H), ACT.Square).then_inc(squares_ready, 1)
                for n in weights_due(g, u):
                    act.wait_ge(ffn_w_turned, n + 1)
                    copy(w_part(n, 0), w_bank(n)).then_inc(ffn_w_hi, 1)

            run_pipeline(act, iteration)

            act.wait_ge(scale_ready, 1)

            def quantise_x(n, s):
                hold_on_constant(act)
                if not fixed(n) or n >= 2:
                    act.wait_ge(xl_ready, n - 1)
                copy(x16[:, s], xn2_t[:, :, at(n * GW, GW)], C_X).then_inc(x16_ready, 1)
                hold_on_constant(act)
                act.wait_ge(x16_ready, n + 1)
                copy(xh[:, :, at(n * GW, GW)], x16[:, s]).then_inc(xh_ready, 1)

            def keep(n, s, done, kept, also):
                for m in range(MF):
                    hold_on_constant(act)
                    act.wait_ge(done, n * MF + m + 1)
                    copy(big[:, at(n * GF + m * GW, GW)], banks[m]).then_inc(kept, 1)
                    if m == 1 and also is not None:
                        quantise_x(n + 1, s)

            quantise_x(0, 0)
            for n in range(GT):
                act.wait_ge(h2_stored[n], 16 * (TILES // GT))
            keep(0, 1, up_done, up_kept, True)
            keep(1, 0, up_done, up_kept, True)
            with act.Fori(1, GROUPS // 2 - 1) as q:
                for s in range(2):
                    keep(q * 2 + s, 1 - s, up_done, up_kept, True)
            keep(GROUPS - 2, 1, up_done, up_kept, True)
            keep(GROUPS - 1, 0, up_done, up_kept, None)

            def keep_gate(n):
                act.wait_ge(up_quantised, n + 1)
                keep(n, 0, gate_done, gate_kept, None)

            run_groups(act, keep_gate, GROUPS)

            act.activation(table_loader[:], ones[:, 0:1], ACT.Sigmoid)
            act.wait_ge(scale_ready, 3)

            def gate_half(q, s):
                c = s + 1
                if half_due(q, c):
                    hold_on_constant(act)
                    half_wait(act, silu_ready, q, c - SLOTS)
                    copy(g16[c % SLOTS], big[:, at((q * SLOTS + c) * HALF, HALF)], C_GATE
                         ).then_inc(gate_quantised, 1)
                c = s
                if half_due(q, c):
                    hold_on_constant(act)
                    half_wait(act, gate_quantised, q, c)
                    act.activation(sig[:, c % SLOTS], g16[c % SLOTS], ACT.Sigmoid, scale=S_GATE
                                   ).then_inc(sig_ready, 1)
                if steps_on_act(q, c):
                    half_wait(act, sig_ready, q, c)
                    copy(sig_steps[:, c % SLOTS], sig[:, c % SLOTS], SIG_STEPS).then_inc(steps_ready, 1)

            run_halves(act, gate_half)

            act.wait_ge(scale_ready, 4)

            def silu_half(q, s):
                c = s
                if half_due(q, c):
                    hold_on_constant(act)
                    half_wait(act, prod_ready, q, c - SLOTS)
                    copy(g16[c % SLOTS], big[:, at((q * SLOTS + c) * HALF, HALF)], C_SILU
                         ).then_inc(silu_quantised, 1)

            run_halves(act, silu_half)

            act.wait_ge(scale_ready, 5)

            def product_parts(q, s):
                for half in range(2):
                    c = 2 * s + half
                    ms = slice(half * MF // 2, (half + 1) * MF // 2)
                    hold_on_constant(act)
                    half_wait(act, ol_ready, q, c - SLOTS)
                    copy(o16[:, s, ms].rearrange("p m n -> p (m n)"),
                         big[:, at((q * SLOTS + c) * HALF, HALF)], C_PROD).then_inc(o16_ready, 1)
                    if half == 0 and (not fixed(q) or q >= 1):
                        act.wait_ge(down_done, q * (2 * GT) + (s - 1) * GT)
                    half_wait(act, o16_ready, q, c)
                    copy(oh[:, s, ms], o16[:, s, ms]).then_inc(oh_ready, 1)

            def product_pair(q):
                product_parts(q, 0)
                product_parts(q, 1)

            run_groups(act, product_pair, GROUPS // 2)


        @block.vector
        def _(dve):
            chain = [0]

            def link(ins):
                chain[0] += 1
                ins.then_inc(dve_chain, 1)
                dve.wait_ge(dve_chain, chain[0])

            barriers = [0]

            def pick_largest(n, bank):
                barriers[0] += 1
                dve.wait_ge(maxima_turned, barriers[0])
                link(dve.tensor_reduce(top[0:n, 0:1], bank[0:n, 0:P], AX.X, ALU.max))
                dve.tensor_scalar(pick[0:n, 0:n], ident[0:n, 0:n], top[0:n, 0:1], None, ALU.mult
                                  ).then_inc(pick_ready, 1)

            def spread_largest(values):
                dve.tensor_reduce(maxima[:, 0:1], values, AX.X, ALU.max).then_inc(maxima_ready, 1)
                pick_largest(1, turn_bank)
                dve.wait_ge(top_spread, barriers[0])
                return turn_bank[:, 0:1]

            def scale_of(largest, units, scale, inverse):
                if units is None:
                    link(dve.tensor_scalar(scale, largest, 1.0 / QMAX_ACT, MIN_SCALE, ALU.mult, ALU.max))
                    dve.reciprocal(inverse, scale).then_inc(scale_ready, 1)
                    return
                link(dve.tensor_scalar(T0, largest, units, 1.0 / QMAX_ACT, ALU.mult, ALU.mult))
                link(dve.tensor_scalar(scale, T0, MIN_SCALE, None, ALU.max))
                link(dve.reciprocal(T1, scale))
                dve.tensor_scalar(inverse, T1, units, None, ALU.mult).then_inc(scale_ready, 1)

            dve.wait_ge(x_loaded, 16)
            dve.tensor_copy(idx_rows, idx_raw).then_inc(idx_rows_ready, 1)
            dve.wait_ge(idx_turned, 1)
            dve.tensor_copy(idx[:].rearrange("p (c b) -> p b c", b=B),
                            turn_bank[:, 0:TILES].rearrange("p (b c) -> p b c", b=B)).then_inc(idx_ready, 1)

            dve.wait_ge(attn_w_loaded, 16 * (1 + 4 + HG))
            dve.tensor_scalar(lora_b2[0:R, :], lora_b2[0:R, :], LORA_SCALING, None, ALU.mult
                              ).then_inc(lora_b_ready, 1)
            dve.wait_ge(attn_w_turned, 4)
            dve.tensor_scalar(wo_t, banks[3].rearrange("p (k n) -> p k n", k=KD), norm_col, None, ALU.mult
                              ).then_inc(wo_ready, 1)

            blocks = ffn_nat.rearrange("p (b q) -> p b q", q=QBLOCK)
            step, rstep, fstep = blk[:, 0], blk[:, 1], blk[:, 2]

            def block_maxima():
                dve.wait_ge(ffn_w_loaded, 16 * 3)
                link(dve.tensor_reduce(step, blocks, AX.X, ALU.max, apply_absolute_value=True))
                dve.tensor_reduce(maxima[:, 0:3], step.rearrange("p (w b) -> p w b", w=3), AX.X, ALU.max
                                  ).then_inc(maxima_ready, 1)

            def matrix_scales():
                dve.wait_ge(top_spread, 1)
                dve.tensor_scalar(TO_F16, banks[0][:, 0:3], MIN_SCALE * QMAX_W, None, ALU.max
                                  ).then_inc(ffn_scales_ready, 1)
                dve.wait_ge(ffn_scales_ready, 1)
                link(dve.tensor_scalar(EXP, TO_F16.bitcast(I32), 0x7F800000, None, ALU.bitwise_and))
                link(dve.tensor_scalar(FROM_F16, EXP.bitcast(F32), 2.0**-14, None, ALU.mult))
                link(dve.tensor_scalar(EXP, TO_F16.bitcast(I32), 23, 0xFF, ALU.logical_shift_right,
                                       ALU.bitwise_xor))
                link(dve.tensor_scalar(EXP, EXP, 23, None, ALU.logical_shift_left))
                link(dve.tensor_scalar(TO_F16, EXP.bitcast(F32), 2.0**13, None, ALU.mult))
                link(dve.tensor_scalar(step, step, 1.0 / QMAX_W, MIN_SCALE, ALU.mult, ALU.max))
                for w in range(3):
                    part = slice(w * NBLK // 3, (w + 1) * NBLK // 3)
                    dve.tensor_scalar(fstep[:, part], step[:, part], TO_F16[:, w:w + 1], None, ALU.mult)
                link(dve.reciprocal(rstep, step))

            def times_step(w, s):
                mine = slice(w * NBLK // 3, (w + 1) * NBLK // 3)
                return dve.tensor_tensor(blocks[:, mine], blocks[:, mine],
                                         s[:, mine].unsqueeze(2).to_broadcast([P, NBLK // 3, QBLOCK]), ALU.mult)

            def rounded(w):
                link(times_step(w, rstep))
                link(dve.tensor_scalar(ffn_nat[:, w * KD * FF:(w + 1) * KD * FF],
                                       ffn_nat[:, w * KD * FF:(w + 1) * KD * FF], ROUNDER, -ROUNDER,
                                       ALU.add, ALU.add))

            weight_steps = {-1: block_maxima, 0: matrix_scales}
            for w in range(3):
                weight_steps[1 + w] = lambda w=w: rounded(w)
                weight_steps[TILES - GT + w] = lambda w=w: times_step(w, fstep).then_inc(ffn_w_quantised, 1)
            dve.wait_ge(consts_ready, 1)

            def norm_stats(g, c, which, ready, first, second, third):
                hold_on_constant(dve)
                tile_wait(dve, ready, g, c)
                dve.bn_stats(stats6[:, which], h_all[:, at(g * GT + c, 1), :].rearrange("p o d -> p (o d)")
                             ).then_inc(first, 1)
                hold_on_constant(dve)
                tile_wait(dve, first, g, c)
                dve.bn_aggr(meanvar[:, c % 2, which], stats6[:, which]).then_inc(second, 1)
                tile_wait(dve, second, g, c)
                dve.tensor_scalar(vareps[:, c % 2, which:which + 1], meanvar[:, c % 2, which, 1:2], NORM_EPS,
                                  None, ALU.add).then_inc(third, 1)

            def normed(g, c, which, dst, ready, done):
                tile_wait(dve, ready, g, c)
                dve.tensor_scalar(dst[:, c % 2:c % 2 + 1], h_all[:, at(g * GT + c, 1), :],
                                  meanvar[:, c % 2, which, 0:1], rstd[:, c % 2, which:which + 1],
                                  ALU.subtract, ALU.mult).then_inc(done, 1)

            o_bank = lo_bank[:, 0:H * DV].rearrange("p (h d) -> p h d", h=H)

            def iteration(g, u):
                c = u - 3
                if due(g, c):
                    tile_wait(dve, onorm_ready, g, c)
                    dve.tensor_tensor(o_n[:, c % 2].rearrange("p (h d) -> p h d", h=H), o_bank[:, :, 0:DH],
                                      onorm[:, c % 2].unsqueeze(2).to_broadcast([P, H, DH]), ALU.mult
                                      ).then_inc(o_n_ready, 1)
                c = u
                if due(g, c):
                    tile_wait(dve, v_done, g, c)
                    dve.tensor_copy(v_ring[:, c % GT, :, 0:DH],
                                    vws_bank[:, 0:D].rearrange("p (h d) -> p h d", h=H)).then_inc(v_ready, 1)
                c = u + 1
                if due(g, c):
                    slot_wait(dve, gathered[c % GT], g, c, 32)
                    tile_wait(dve, lora_done, g, c)
                    dve.tensor_tensor(h_all[:, at(g * GT + c, 1), :], base_ring[:, c % GT:c % GT + 1, :],
                                      lo_bank[:, 0:D].unsqueeze(1), ALU.add).then_inc(h_ready, 1)
                    norm_stats(g, c, 0, h_ready, stats_done, meanvar_done, vareps_ready)
                if fixed(g) and GT * g + u == 0:
                    pick_largest(3, banks[0])
                c = u - 4
                if due(g, c):
                    hold_on_constant(dve)
                    tile_wait(dve, xn2_t_ready, g, c)
                    dve.tensor_reduce(absmax[:, at(g * GT + c, 1)], xn2_t[:, :, at((g * GT + c) * P, P)],
                                      AX.XY, ALU.max, apply_absolute_value=True).then_inc(absmax_ready, 1)
                c = u + 1
                if due(g, c):
                    normed(g, c, 0, xn, rstd_ready, xn_ready)
                c = u - 1
                if due(g, c):
                    tile_wait(dve, scores_done, g, c)
                    for half in range(2):
                        r = slice(2 * half, 2 * half + 2)
                        dve.tensor_tensor(probs[:, c % 2, r].rearrange("p r n t -> p r (n t)"),
                                          scores_ps[:, r, 0:NG * P], causal.rearrange("p (r n) -> p r n", r=2),
                                          ALU.mult).then_inc(probs_ready, 1)
                c = u - 3
                if due(g, c):
                    tile_wait(dve, attn_done, g, c)
                    dve.tensor_tensor(h_all[:, at(g * GT + c, 1), :], h_all[:, at(g * GT + c, 1), :],
                                      vws_bank[:, 0:D].unsqueeze(1), ALU.add).then_inc(h2_ready, 1)
                    norm_stats(g, c, 1, h2_ready, stats2_done, meanvar2_done, vareps2_ready)
                c = u - 2
                if due(g, c):
                    tile_wait(dve, squares_ready, g, c)
                    dve.tensor_scalar(denom2[:].unsqueeze(2), squares[:, c % 2, :, DH:DV], 1.0, NORM_EPS,
                                      ALU.max, ALU.mult).then_inc(denom2_done, 1)
                    dve.tensor_reduce(ssq[:], squares[:, c % 2, :, 0:DH], AX.X, ALU.add).then_inc(ssq_done, 1)
                    tile_wait(dve, ssq_done, g, c)
                    tile_wait(dve, denom2_done, g, c)
                    dve.scalar_tensor_tensor(out=meansq[:, c % 2], in0=ssq[:], scalar=1.0 / DH, in1=denom2[:],
                                             op0=ALU.mult, op1=ALU.add).then_inc(meansq_ready, 1)
                    tile_wait(dve, state_done, g, c)
                    dve.tensor_tensor(state_new[:, c % 2], vws_bank[:, 0:NG * SW].rearrange(
                        "p (n w) -> p n w", n=NG), diag, ALU.mult).then_inc(state_masked, 1)
                c = u - 3
                if due(g, c):
                    normed(g, c, 1, xn2, rstd2_ready, xn2_ready)
                if fixed(g) and GT * g + u in weight_steps:
                    weight_steps[GT * g + u]()
                for n in weights_due(g, u):
                    dve.wait_ge(ffn_w_hi, n + 1)
                    dve.tensor_tensor(w_part(n, 1), w_bank(n), w_part(n, 0), ALU.subtract).then_inc(ffn_w_lo, 1)

            run_pipeline(dve, iteration)

            dve.wait_ge(absmax_ready, TILES)
            largest = spread_largest(absmax[:, 0:TILES])
            scale_of(largest, None, S_X, C_X)

            def low_x(n, s):
                dve.wait_ge(xh_ready, n + 1)
                dve.tensor_tensor(xl[:, :, at(n * GW, GW)], x16[:, s], xh[:, :, at(n * GW, GW)], ALU.subtract
                                  ).then_inc(xl_ready, 1)

            def group_max(n, kept, done, pieces=(3, 3)):
                k = 0
                for piece in pieces:
                    hold_on_constant(dve)
                    dve.wait_ge(kept, n * MF + (k + piece))
                    dve.tensor_reduce(absmax[:, at(n * MF + k, piece)],
                                      big[:, at(n * GF + k * GW, piece * GW)].rearrange("p (m n) -> p m n", m=piece),
                                      AX.X, ALU.max, apply_absolute_value=True).then_inc(done, 1)
                    k += piece

            last_pieces = (3, 2, 1)

            low_x(0, 0)
            low_x(1, 1)
            group_max(0, up_kept, up_max)
            low_x(2, 0)
            group_max(1, up_kept, up_max)
            with dve.Fori(1, GROUPS // 2 - 1) as q:
                for s in range(2):
                    low_x(q * 2 + (s + 1), 1 - s)
                    group_max(q * 2 + s, up_kept, up_max)
            low_x(GROUPS - 1, 1)
            group_max(GROUPS - 2, up_kept, up_max)
            group_max(GROUPS - 1, up_kept, up_max, last_pieces)
            dve.wait_ge(up_max, 2 * GROUPS + 1)
            largest = spread_largest(absmax[:])
            link(dve.tensor_scalar(S_PROD, S_X, FROM_F16[:, 0:1], None, ALU.mult))
            scale_of(largest, S_PROD, S_UP, C_UP)
            dve.wait_ge(scale_ready, 2)

            def quantise_up(n):
                dve.tensor_scalar(quant[:, at(n * GF, GF)], big[:, at(n * GF, GF)], C_UP, None, ALU.mult
                                  ).then_inc(up_quantised, 1)

            def up_and_gate(n):
                quantise_up(n)
                group_max(n, gate_kept, gate_max)

            run_groups(dve, up_and_gate, GROUPS - 1)
            quantise_up(GROUPS - 1)
            group_max(GROUPS - 1, gate_kept, gate_max, last_pieces)
            dve.wait_ge(gate_max, 2 * GROUPS + 1)
            largest = spread_largest(absmax[:])
            link(dve.tensor_scalar(S_PROD, S_X, FROM_F16[:, 1:2], None, ALU.mult))
            scale_of(largest, S_PROD, S_GATE, C_GATE)
            dve.wait_ge(scale_ready, 3)
            link(dve.tensor_scalar(S_SIG, S_GATE, 1.0 / SIG_STEPS, None, ALU.mult))

            def half_max(q, c, ready, done):
                hold_on_constant(dve)
                half_wait(dve, ready, q, c)
                dve.tensor_reduce(absmax[:, at(q * SLOTS + c, 1)], big[:, at((q * SLOTS + c) * HALF, HALF)], AX.X,
                                  ALU.max, apply_absolute_value=True).then_inc(done, 1)

            def silu_half(q, s):
                c = s
                mine = half_due(q, c) and not steps_on_act(q, c)
                if mine:
                    half_wait(dve, sig_ready, q, c)
                    slot = (c + 1) // 2 % 2
                    dve.tensor_scalar(sig16[:, slot], sig[:, c], SIG_STEPS, QMAX_SIG, ALU.mult, ALU.min
                                      ).then_inc(sig_quantised, 1)
                if half_due(q, c - 1):
                    half_max(q, c - 1, silu_ready, silu_max)
                if half_due(q, c):
                    dst = big[:, at((q * SLOTS + c) * HALF, HALF)]
                    if mine:
                        dve.wait_ge(sig_quantised, q * (SLOTS // 2) + ((c + 1) // 2 + 1))
                        dve.tensor_tensor(dst, sig16[:, slot], g16[c], ALU.mult).then_inc(silu_ready, 1)
                    else:
                        dve.wait_ge(steps_ready, q * (SLOTS // 2) + (c // 2 + 1))
                        dve.scalar_tensor_tensor(out=dst, in0=sig_steps[:, c], scalar=QMAX_SIG, in1=g16[c],
                                                 op0=ALU.min, op1=ALU.mult).then_inc(silu_ready, 1)

            run_halves(dve, silu_half)
            dve.wait_ge(silu_max, 2 * GROUPS)
            largest = spread_largest(absmax[:, 0:HALVES])
            scale_of(largest, S_SIG, S_SILU, C_SILU)

            def product_half(q, s):
                c = s
                if half_due(q, c):
                    half_wait(dve, silu_quantised, q, c)
                    dve.tensor_tensor(big[:, at((q * SLOTS + c) * HALF, HALF)], g16[c],
                                      quant[:, at((q * SLOTS + c) * HALF, HALF)], ALU.mult
                                      ).then_inc(prod_ready, 1)
                if half_due(q, c - 1):
                    half_max(q, c - 1, prod_ready, prod_max)

            run_halves(dve, product_half)
            dve.wait_ge(prod_max, 2 * GROUPS)
            largest = spread_largest(absmax[:, 0:HALVES])
            dve.wait_ge(scale_ready, 4)
            link(dve.tensor_scalar(T1, S_SILU, S_UP, None, ALU.mult))
            link(dve.tensor_copy(S_SIG, T1))
            scale_of(largest, S_SIG, S_PROD, C_PROD)
            dve.wait_ge(scale_ready, 5)
            link(dve.tensor_scalar(S_OUT, S_PROD, FROM_F16[:, 2:3], None, ALU.mult))

            def low_product(q, s):
                for half in range(2):
                    ms = slice(half * MF // 2, (half + 1) * MF // 2)
                    half_wait(dve, oh_ready, q, 2 * s + half)
                    dve.tensor_tensor(ol[:, s % 2, ms], o16[:, s % 2, ms], oh[:, s % 2, ms], ALU.subtract
                                      ).then_inc(ol_ready, 1)

            def finish(q, s):
                dve.wait_ge(res_loaded[s], q * 16 + 16)
                for t in range(GT):
                    dve.wait_ge(down_done, q * (2 * GT) + (s * GT + t + 1))
                    dve.scalar_tensor_tensor(out=res[:, s, t], in0=banks[(s * GT + t) % 8][:, 0:D],
                                             scalar=S_OUT, in1=res[:, s, t], op0=ALU.mult, op1=ALU.add
                                             ).then_inc(out_ready, 1)

            low_product(0, 0)
            with dve.Fori(0, GROUPS // 2 - 1) as q:
                for s in range(2):
                    low_product(q, s + 1)
                    finish(q, s)
            low_product(GROUPS // 2 - 1, 1)
            finish(GROUPS // 2 - 1, 0)
            finish(GROUPS // 2 - 1, 1)

        @block.tensor
        def _(pe):
            barriers = [0]

            def turn_maxima(n, bank):
                barriers[0] += 1
                pe.wait_ge(maxima_ready, barriers[0])
                pe.transpose(bank[0:n, 0:P], maxima[:, 0:n], ident[:]).then_inc(maxima_turned, 1)

            def spread_pick(n, bank):
                pe.wait_ge(pick_ready, barriers[0])
                pe.matmul(bank[:, 0:n], ones[0:n, :], pick[0:n, 0:n], start=True, stop=True
                          ).then_inc(top_spread, 1)

            def spread_largest():
                turn_maxima(1, turn_bank)
                spread_pick(1, turn_bank)

            pe.wait_ge(ident_ready, 1)
            pe.wait_ge(idx_rows_ready, 1)
            pe.transpose(turn_bank[:, 0:TILES], idx_rows, ident[0:TILES, 0:TILES]).then_inc(idx_turned, 1)
            pe.wait_ge(attn_w_loaded, 16 * (1 + 4 + HG))
            for n in range(4):
                for k in range(KD):
                    for o in range(OT):
                        last = pe.transpose(banks[n][:, k * D + o * P:k * D + (o + 1) * P],
                                            attn_nat[:, n, o, k * P:(k + 1) * P], ident[:])
                last.then_inc(attn_w_turned, 1)
            pe.wait_ge(consts_ready, 1)

            def turn_weights(n):
                which, k0 = n // 3, 2 * (n % 3)
                nat = ffn_nat[:, which * KD * FF:(which + 1) * KD * FF]
                for a in range(2):
                    for b in range(2):
                        if which < 2:
                            src = nat.rearrange("p (o n) -> p o n", n=D)[:, k0 + b, a * P:(a + 1) * P]
                        else:
                            src = nat.rearrange("p (o n) -> p o n", n=FF)[:, b, (k0 + a) * P:(k0 + a + 1) * P]
                        last = pe.transpose(w_bank(n)[:, a, b * P:(b + 1) * P], src, ident[:])
                last.then_inc(ffn_w_turned, 1)

            pe.wait_ge(lora_b_ready, 1)
            pe.wait_ge(qkv_w_ready, 3)
            pe.wait_ge(wo_ready, 1)
            pe.wait_ge(idx_ready, 1)

            def iteration(g, u):
                c = u
                if due(g, c):
                    tile_wait(pe, xn_t_ready, g, c)
                    tile_wait(pe, qkt_ready, g, c - 1)
                    for k in range(KD):
                        last = pe.matmul(qk_bank[:], xn_t[:, c % 2, k], wqkv_t[:, k, 0:2 * D],
                                         start=(k == 0), stop=(k == KD - 1))
                    last.then_inc(qk_done, 1)
                    tile_wait(pe, state_masked, g, c - 3)
                    for k in range(KD):
                        last = pe.matmul(vws_bank[:, 0:D], xn_t[:, c % 2, k], wqkv_t[:, k, 2 * D:3 * D],
                                         start=(k == 0), stop=(k == KD - 1))
                    last.then_inc(v_done, 1)
                if fixed(g) and GT * g + u == 0:
                    turn_maxima(3, banks[0])
                def scores(n):
                    tile_wait(pe, qkt_ready, g, u - 1)
                    tile_wait(pe, probs_ready, g, u - 2, 2)
                    if fixed(g) and GT * g + u == 1:
                        pe.wait_ge(ffn_scales_ready, 1)
                    for r in range(HG):
                        rows = slice(r * DH, (r + 1) * DH)
                        last = pe.matmul(scores_ps[:, r, n * P:(n + 1) * P], qkt_ring[rows, (u - 1) % GT, NG + n],
                                         qkt_ring[rows, (u - 1) % GT, n], start=True, stop=True)
                    if n == NG - 1:
                        last.then_inc(scores_done, 1)

                if due(g, u - 1):
                    scores(0)
                if due(g, u - 3) or due(g, u - 4):
                    tile_wait(pe, lora_t_ready, g, u + 1)
                    tile_wait(pe, xn_t_ready, g, u)
                    if fixed(g):
                        tile_wait(pe, o_t_ready, g, u - 4)
                        tile_wait(pe, xn2_t_ready, g, u - 5)
                c = u - 4
                if due(g, c):
                    tile_wait(pe, xn2_ready, g, c)
                    for k in range(KD):
                        last = pe.transpose(turn_bank[:, (KD + k) * P:(KD + k + 1) * P],
                                            xn2[:, c % 2, k * P:(k + 1) * P], ident[:])
                    last.then_inc(xn2_turned, 1)
                c = u - 3
                if due(g, c):
                    tile_wait(pe, o_n_ready, g, c)
                    for k in range(KD):
                        last = pe.transpose(turn_bank[:, k * P:(k + 1) * P], o_n[:, c % 2, k * P:(k + 1) * P],
                                            ident[:])
                    last.then_inc(o_turned, 1)
                c = u + 1
                if due(g, c):
                    tile_wait(pe, lora_t_ready, g, c)
                    pe.matmul(lo_bank[:, 0:D], lora_t[0:R, c % 2], lora_b2[0:R, :], start=True, stop=True
                              ).then_inc(lora_done, 1)
                if fixed(g) and GT * g + u == 0:
                    spread_pick(3, banks[0])
                if due(g, u - 1):
                    scores(1)
                c = u - 3
                if due(g, c):
                    tile_wait(pe, o_t_ready, g, c)
                    tile_wait(pe, v_ready, g, u)
                    if fixed(g):
                        tile_wait(pe, state_masked, g, c)
                    for k in range(KD):
                        last = pe.matmul(vws_bank[:, 0:D], o_t[:, c % 2, k], wo_t[:, k], start=(k == 0),
                                         stop=(k == KD - 1))
                    last.then_inc(attn_done, 1)
                c = u
                if due(g, c):
                    tile_wait(pe, qk_ready, g, c)
                    for n in range(2 * NG):
                        last = pe.transpose(qk_bank[:, n * P:(n + 1) * P], qk_ring[:, c % GT, n * P:(n + 1) * P],
                                            ident[:])
                    last.then_inc(qk_turned, 1)

                def attend(heads):
                    tile_wait(pe, probs_ready, g, u - 2, 2)
                    tile_wait(pe, v_ready, g, u - 2)
                    for h in heads:
                        last = pe.matmul(lo_bank[:, h * DV:(h + 1) * DV], probs[:, (u - 2) % 2, h % HG, h // HG],
                                         v_ring[:, (u - 2) % GT, h], start=False, stop=(h == H - 1),
                                         skip_group_check=True)
                    return last

                c = u - 2
                if due(g, c):
                    tile_wait(pe, state_ready, g, u - 4)
                    tile_wait(pe, h_ready, g, u + 1)
                    if fixed(g):
                        tile_wait(pe, o_n_ready, g, u - 3)
                    for n in range(NG):
                        pe.matmul(lo_bank[:, n * SW:(n + 1) * SW], qkt_ring[:, c % GT, n], state[:, c % B, n],
                                  start=(n == 0), stop=False, skip_group_check=True)
                    attend(range(H // 2))

                def free_turn_bank():
                    tile_wait(pe, xn2_t_ready, g, u - 4)
                    if fixed(g):
                        tile_wait(pe, o_t_ready, g, u - 3)
                        tile_wait(pe, lora_t_ready, g, u + 1)
                        tile_wait(pe, xn_t_ready, g, u)

                c = u + 2
                if due(g, c):
                    hold_on_constant(pe)
                    slot_wait(pe, gathered[c % GT], g, c, 32)
                    free_turn_bank()
                    pe.transpose(turn_bank[0:R, KD * P:KD * P + P], lora_ring[:, c % GT], ident[:]
                                 ).then_inc(lora_turned, 1)
                c = u + 1
                if due(g, c):
                    tile_wait(pe, xn_ready, g, c)
                    free_turn_bank()
                    for k in range(KD):
                        last = pe.transpose(turn_bank[:, k * P:(k + 1) * P], xn[:, c % 2, k * P:(k + 1) * P],
                                            ident[:])
                    last.then_inc(xn_turned, 1)
                c = u - 2
                if due(g, c):
                    attend(range(H // 2, H)).then_inc(o_done, 1)
                    tile_wait(pe, h2_ready, g, u - 3)
                    if fixed(g):
                        tile_wait(pe, v_ready, g, u)
                    for n in range(NG):
                        last = pe.matmul(vws_bank[:, n * SW:(n + 1) * SW],
                                         qk_ring[:, c % GT, D + n * P:D + (n + 1) * P],
                                         v_ring[:, c % GT, n * HG:(n + 1) * HG].rearrange("p h d -> p (h d)"),
                                         start=(n == 0), stop=(n == NG - 1), skip_group_check=True)
                    last.then_inc(state_done, 1)
                for n in weights_due(g, u):
                    pe.wait_ge(ffn_w_quantised, 3)
                    pe.wait_ge(probs_ready, 2 * TILES)
                    if n >= HG:
                        pe.wait_ge(ffn_w_lo, n - HG + 1)
                    turn_weights(n)

            run_pipeline(pe, iteration)

            def project(n, m, hi, lo, done):
                for k in range(KD):
                    cols = slice(m * P, (m + 1) * P)
                    xs = at(n * GW, GW)
                    pe.matmul(banks[m], hi[:, k, cols], xh[:, k, xs], start=(k == 0), stop=False)
                    pe.matmul(banks[m], hi[:, k, cols], xl[:, k, xs], start=False, stop=False)
                    last = pe.matmul(banks[m], lo[:, k, cols], xh[:, k, xs], start=False, stop=(k == KD - 1))
                last.then_inc(done, 1)

            spread_largest()
            pe.wait_ge(ffn_w_lo, 9)

            def up_group(n):
                pe.wait_ge(xl_ready, n + 1)
                for m in range(MF):
                    if not fixed(n) or n >= 1:
                        pe.wait_ge(up_kept, n * MF + (m + 1 - MF))
                    project(n, m, up_hi, up_lo, up_done)

            run_groups(pe, up_group, GROUPS)

            def gate_group(n):
                for m in range(MF):
                    if fixed(n) and n == 0:
                        pe.wait_ge(up_kept, (GROUPS - 1) * MF + m + 1)
                    else:
                        pe.wait_ge(gate_kept, n * MF + (m + 1 - MF))
                    project(n, m, gate_hi, gate_lo, gate_done)
                    if fixed(n) and m == 1:
                        spread_largest()

            run_groups(pe, gate_group, GROUPS)
            for _ in range(3):
                spread_largest()
            pe.wait_ge(gate_kept, GROUPS * MF)
            pe.wait_ge(scale_ready, 5)

            def down_pair(q):
                for s in range(2):
                    for half in range(2):
                        half_wait(pe, ol_ready, q, 2 * s + half)
                        for t in range(GT):
                            bank = banks[s * GT + t]
                            if half == 0 and (not fixed(q) or q >= 1):
                                pe.wait_ge(out_ready, q * (2 * GT) + (s * GT + t + 1 - 2 * GT))
                            ts = slice(t * P, (t + 1) * P)
                            for m in range(half * MF // 2, (half + 1) * MF // 2):
                                pe.matmul(bank[:, 0:D], oh[:, s, m, ts], down_hi[:, m], start=(m == 0), stop=False)
                                pe.matmul(bank[:, 0:D], oh[:, s, m, ts], down_lo[:, m], start=False, stop=False)
                                last = pe.matmul(bank[:, 0:D], ol[:, s, m, ts], down_hi[:, m], start=False,
                                                 stop=(m == MF - 1))
                            if half:
                                last.then_inc(down_done, 1)

            run_groups(pe, down_pair, GROUPS // 2)


_INS = ["x", "L0_tok_base_weight", "L0_tok_lora_A", "L0_tok_lora_B", "L0_attn_Wq", "L0_attn_Wk", "L0_attn_Wv",
        "L0_attn_Wo", "L0_attn_norm_w", "L0_ffn_w_gate", "L0_ffn_w_up", "L0_ffn_w_down"]


def kernel(**inputs):
    import numpy as _np
    import concourse.bacc as _bacc
    from concourse import mybir as _mybir
    from concourse.bass_utils import run_bass_kernel_spmd as _run

    nc = _bacc.Bacc("TRN2", target_bir_lowering=False, num_devices=1)
    arrays, args = {}, []
    for name in _INS:
        a = _np.ascontiguousarray(inputs[name])
        arrays[f"in_{name}"] = a
        args.append(nc.dram_tensor(f"in_{name}", a.shape, _mybir.dt.from_np(a.dtype), kind="ExternalInput").ap())
    batch, length = inputs["x"].shape
    width = inputs["L0_tok_base_weight"].shape[1]
    args.append(nc.dram_tensor("out_h", (batch, length, width), _mybir.dt.float32, kind="ExternalOutput").ap())
    lm_tower(nc, *args)
    r = _run(nc, [arrays], core_ids=[0])
    return r.results[0]["out_h"]
```

```python
from contextlib import ExitStack

import concourse.bass as bass
from concourse import mybir

ALU = mybir.AluOpType
ACT = mybir.ActivationFunctionType
AX = mybir.AxisListType
F32 = mybir.dt.float32
F16 = mybir.dt.float16
I16 = mybir.dt.int16
U16 = mybir.dt.uint16
I32 = mybir.dt.int32

P = 128
NORM_EPS = 1e-5
LORA_SCALING = 2.0
QMAX_ACT = 2.0**15 - 1.0
QMAX_W = 2.0**3 - 1.0
QMAX_SIG = 65535.0
SIG_STEPS = 65536.0
MIN_SCALE = 1e-12
QBLOCK = 32
ROUNDER = 12582912.0
NORMED_TO_F16 = 2.0**10


def lm_tower(nc, x, base, lora_a, lora_b, wq, wk, wv, wo, norm_w, w_gate, w_up, w_down, out):
    B, S = x.shape
    D = base.shape[1]
    R = lora_a.shape[1]
    DH = norm_w.shape[0]
    H = D // DH
    FF = w_gate.shape[0]
    TILES = B * S // P
    CHUNKS = S // P
    KD = D // P
    MF = FF // P
    HG = P // DH
    NG = H // HG
    DV = DH + 1
    SW = HG * DV
    GT = 4
    GW = GT * P
    GROUPS = TILES // GT
    GF = MF * GW
    HALF = GF // 2
    OT = D // P
    SLOTS = 4
    HALVES = 2 * GROUPS
    assert B == 2 and KD == 2 and NG == 2 and MF % 3 == 0 and TILES % GT == 0 and R <= 32

    h2_dram = nc.dram_tensor("h2_kept", (TILES, P, D), F32, kind="Internal").ap()

    with ExitStack() as ctx:
        def sb(name, shape, dt=F32):
            return ctx.enter_context(nc.sbuf_tensor(name, shape, dt))

        def sem(name):
            return ctx.enter_context(nc.semaphore(name))

        big = sb("big", [P, GROUPS * GF])
        quant = sb("quant", [P, GROUPS * GF], I16)
        xregion = sb("xregion", [P, 2 * KD * TILES * P], F16)
        ident = sb("ident", [P, P])
        ones = sb("ones", [P, P])
        minus_half = sb("minus_half", [P, H])
        up_hi = sb("up_hi", [P, KD, FF], F16)
        up_lo = sb("up_lo", [P, KD, FF], F16)
        gate_hi = sb("gate_hi", [P, KD, FF], F16)
        gate_lo = sb("gate_lo", [P, KD, FF], F16)
        down_hi = sb("down_hi", [P, MF, D], F16)
        down_lo = sb("down_lo", [P, MF, D], F16)
        absmax = sb("absmax", [P, GROUPS * MF])
        maxima = sb("maxima", [P, 4])
        top = sb("top", [P, 4])
        pick = sb("pick", [P, 4])
        scales = sb("scales", [P, 32])
        idx = sb("idx", [P, TILES], I32)
        table_loader = sb("table_loader", [P, 1])
        idx_slot = sb("idx_slot", [P, GT], I32)
        stats6 = sb("stats6", [P, 2, 6])
        meanvar = sb("meanvar", [P, 2, 2, 2])
        vareps = sb("vareps", [P, 2, 2])
        rstd = sb("rstd", [P, 2, 2])
        ssq = sb("ssq", [P, H])
        denom2 = sb("denom2", [P, H])
        meansq = sb("meansq", [P, 2, H])
        onorm = sb("onorm", [P, 2, H])

        big_at = [0]

        def in_big(shape):
            n = 1
            for k in shape:
                n *= k
            v = big[:, big_at[0]:big_at[0] + n]
            big_at[0] += n
            assert big_at[0] <= GROUPS * GF
            names = "abcd"[:len(shape)]
            if len(shape) == 1:
                return v
            return v.rearrange(f"p ({' '.join(names)}) -> p {' '.join(names)}",
                               **{c: k for c, k in zip(names[1:], shape[1:])})

        h_all = in_big([TILES, D])
        base_ring = in_big([GT, D])
        lora_ring = in_big([GT, R])
        lora_t = in_big([2, P])
        xn = in_big([2, D])
        xn_t = in_big([2 * KD * P]).bitcast(F16).rearrange("p (s a k n) -> p s a k n", s=2, a=2, k=KD)
        k_ring = in_big([GT, D])
        v_ring = in_big([GT, H, DV])
        qkt_ring = in_big([GT, 2 * NG, P])
        probs = in_big([2, HG, NG, P])
        state = in_big([B, NG, SW])
        state_new = in_big([2, NG, SW])
        diag = in_big([NG, SW])
        squares = in_big([2, H, DV])
        o_n = in_big([2, D])
        o_t = in_big([2 * KD * P]).bitcast(F16).rearrange("p (s a k n) -> p s a k n", s=2, a=2, k=KD)
        xn2 = in_big([2, D])

        xreg32 = xregion[:].bitcast(F32)
        x_at = [0]

        def in_x(n):
            v = xreg32[:, x_at[0]:x_at[0] + n]
            x_at[0] += n
            assert x_at[0] <= KD * TILES * P
            return v

        wq_t = in_x(KD * D).bitcast(F16).rearrange("p (a k n) -> p a k n", a=2, k=KD)
        wkv_t = in_x(KD * 2 * D).bitcast(F16).rearrange("p (a k n) -> p a k n", a=2, k=KD)
        wo_t = in_x(KD * D).bitcast(F16).rearrange("p (a k n) -> p a k n", a=2, k=KD)
        wo_normed = in_x(KD * D).rearrange("p (k n) -> p k n", k=KD)
        lora_b2 = in_x(D)
        causal = in_x(2 * NG * P)
        norm_col = in_x(1)
        ffn_nat = in_x(3 * KD * FF)
        quant32 = quant[:].bitcast(F32)
        xn2_t = quant32[:, 0:KD * TILES * P].rearrange("p (k n) -> p k n", k=KD)
        attn_nat = quant32[:, KD * TILES * P:KD * TILES * P + 4 * KD * D].rearrange(
            "p (w k n) -> p w k n", w=4, k=KD)
        x16 = quant[:, 2 * KD * TILES * P:2 * KD * TILES * P + 2 * KD * GW].rearrange(
            "p (s k n) -> p s k n", s=2, k=KD)
        NBLK = 3 * KD * FF // QBLOCK
        blk = big[:, big_at[0]:big_at[0] + 3 * NBLK].rearrange("p (a b) -> p a b", a=3)
        idx_rows = big[0:TILES, big_at[0] + 3 * NBLK:big_at[0] + 3 * NBLK + P]
        idx_raw = big[0:TILES, big_at[0] + 3 * NBLK + P:big_at[0] + 3 * NBLK + 2 * P].bitcast(I32)

        xh = xregion[:, 0:KD * TILES * P].rearrange("p (k n) -> p k n", k=KD)
        xl = xregion[:, KD * TILES * P:2 * KD * TILES * P].rearrange("p (k n) -> p k n", k=KD)
        assert KD * FF == HALF
        g16 = [w[:].rearrange("p k n -> p (k n)").bitcast(I16) for w in (up_hi, up_lo, gate_hi, gate_lo)]
        sig = xregion[:, 0:8 * HALF].bitcast(F32).rearrange("p (s n) -> p s n", s=SLOTS)
        sig_steps = xregion[:, 0:8 * HALF].bitcast(I32).rearrange("p (s n) -> p s n", s=SLOTS)
        sig16 = xregion[:, 8 * HALF:10 * HALF].bitcast(U16).rearrange("p (s n) -> p s n", s=2)
        oh = xregion[:, 0:2 * GF].rearrange("p (s m n) -> p s m n", s=2, m=MF)
        ol = xregion[:, 2 * GF:4 * GF].rearrange("p (s m n) -> p s m n", s=2, m=MF)
        res = xregion[:, 4 * GF:4 * GF + 4 * GT * D].bitcast(F32).rearrange(
            "p (s t d) -> p s t d", s=2, t=GT)
        o16 = quant[:, 0:2 * GF].rearrange("p (s m n) -> p s m n", s=2, m=MF)

        scores_ps = ctx.enter_context(nc.psum_tensor("scores_ps", [P, HG, 512], F32))
        kv_bank = ctx.enter_context(nc.psum_tensor("kv_bank", [P, 512], F32))
        qws_bank = ctx.enter_context(nc.psum_tensor("qws_bank", [P, 512], F32))
        lo_bank = ctx.enter_context(nc.psum_tensor("lo_bank", [P, 512], F32))
        turn_bank = ctx.enter_context(nc.psum_tensor("turn_bank", [P, 512], F32))
        banks = [scores_ps[:, n, :] for n in range(HG)] + [kv_bank[:], qws_bank[:], lo_bank[:], turn_bank[:]]

        x_loaded = sem("x_loaded")
        attn_w_loaded = sem("attn_w_loaded")
        ffn_w_loaded = sem("ffn_w_loaded")
        ident_ready = sem("ident_ready")
        consts_ready = sem("consts_ready")
        pool_chain = sem("pool_chain")
        idx_rows_ready = sem("idx_rows_ready")
        idx_turned = sem("idx_turned")
        idx_ready = sem("idx_ready")
        lora_b_ready = sem("lora_b_ready")
        attn_w_turned = sem("attn_w_turned")
        attn_w_hi = sem("attn_w_hi")
        attn_w_lo = sem("attn_w_lo")
        ffn_w_quantised = sem("ffn_w_quantised")
        ffn_w_turned = sem("ffn_w_turned")
        ffn_w_hi = sem("ffn_w_hi")
        ffn_w_lo = sem("ffn_w_lo")
        ffn_maxima_read = sem("ffn_maxima_read")
        steps_ready = sem("steps_ready")
        dve_chain = sem("dve_chain")
        maxima_ready = sem("maxima_ready")
        maxima_turned = sem("maxima_turned")
        pick_ready = sem("pick_ready")
        top_spread = sem("top_spread")
        scale_ready = sem("scale_ready")
        slot_ready = sem("slot_ready")
        gathered = [sem(f"gathered{n}") for n in range(GT)]
        lora_turned = sem("lora_turned")
        lora_t_ready = sem("lora_t_ready")
        lora_done = sem("lora_done")
        h_ready = sem("h_ready")
        stats_done = sem("stats_done")
        meanvar_done = sem("meanvar_done")
        vareps_ready = sem("vareps_ready")
        rstd_ready = sem("rstd_ready")
        xn_ready = sem("xn_ready")
        xn_turned = sem("xn_turned")
        xn_hi_ready = sem("xn_hi_ready")
        kv_done = sem("kv_done")
        k_ready = sem("k_ready")
        q_done = sem("q_done")
        v_ready = sem("v_ready")
        k_turned = sem("k_turned")
        k_t_ready = sem("k_t_ready")
        scores_done = sem("scores_done")
        probs_ready = sem("probs_ready")
        o_done = sem("o_done")
        squares_ready = sem("squares_ready")
        ssq_done = sem("ssq_done")
        denom2_done = sem("denom2_done")
        meansq_ready = sem("meansq_ready")
        onorm_ready = sem("onorm_ready")
        o_n_ready = sem("o_n_ready")
        o_turned = sem("o_turned")
        o_hi_ready = sem("o_hi_ready")
        state_done = sem("state_done")
        state_masked = sem("state_masked")
        state_kept = sem("state_kept")
        state_ready = sem("state_ready")
        attn_done = sem("attn_done")
        h2_ready = sem("h2_ready")
        h2_stored = [sem(f"h2_stored{n}") for n in range(GT)]
        stats2_done = sem("stats2_done")
        meanvar2_done = sem("meanvar2_done")
        vareps2_ready = sem("vareps2_ready")
        rstd2_ready = sem("rstd2_ready")
        xn2_ready = sem("xn2_ready")
        xn2_turned = sem("xn2_turned")
        xn2_t_ready = sem("xn2_t_ready")
        absmax_ready = sem("absmax_ready")
        x16_ready = sem("x16_ready")
        wo_normed_ready = sem("wo_normed_ready")
        attn_scales_ready = sem("attn_scales_ready")
        attn_maxima_read = sem("attn_maxima_read")
        xn_lo_ready = sem("xn_lo_ready")
        o_lo_ready = sem("o_lo_ready")
        q_t_ready = sem("q_t_ready")
        xh_ready = sem("xh_ready")
        xl_ready = sem("xl_ready")
        up_done = sem("up_done")
        up_kept = sem("up_kept")
        up_max = sem("up_max")
        up_quantised = sem("up_quantised")
        gate_done = sem("gate_done")
        gate_kept = sem("gate_kept")
        gate_max = sem("gate_max")
        gate_quantised = sem("gate_quantised")
        sig_ready = sem("sig_ready")
        sig_quantised = sem("sig_quantised")
        silu_ready = sem("silu_ready")
        silu_max = sem("silu_max")
        silu_quantised = sem("silu_quantised")
        prod_ready = sem("prod_ready")
        prod_max = sem("prod_max")
        o16_ready = sem("o16_ready")
        oh_ready = sem("oh_ready")
        ol_ready = sem("ol_ready")
        down_done = sem("down_done")
        res_loaded = [sem(f"res_loaded{n}") for n in range(2)]
        out_ready = sem("out_ready")
        out_stored = [sem(f"out_stored{n}") for n in range(2)]

        def fixed(n):
            return isinstance(n, int)

        def at(start, n):
            return slice(start, start + n) if fixed(start) else bass.ds(start, n)

        def due(g, c):
            return not fixed(g) or 0 <= GT * g + c < TILES

        def tile_wait(eng, s, g, c, per=1):
            if not fixed(g):
                eng.wait_ge(s, g * (GT * per) + (c + 1) * per)
            elif GT * g + c >= 0:
                eng.wait_ge(s, min(GT * g + c + 1, TILES) * per)

        def slot_wait(eng, s, g, c, per):
            eng.wait_ge(s, g * per + (c // GT + 1) * per)

        def hold_on_constant(eng):
            eng.wait_ge(consts_ready, 1)

        def run_pipeline(eng, iteration):
            for i in range(-2, 2 * GT):
                iteration(i // GT, i % GT)
            with eng.Fori(2, TILES // GT - 1) as g:
                for u in range(GT):
                    iteration(g, u)
            for i in range(TILES - GT, TILES + 5):
                iteration(i // GT, i % GT)

        def half_due(q, c):
            return not fixed(q) or 0 <= SLOTS * q + c < HALVES

        def half_wait(eng, s, q, c):
            if not fixed(q) or SLOTS * q + c >= 0:
                eng.wait_ge(s, q * SLOTS + (c + 1))

        def steps_on_act(q, c):
            return c % 2 == 1 and half_due(q, c) and not (fixed(q) and SLOTS * q + c == HALVES - 1)

        def run_halves(eng, half):
            for c in range(-1, SLOTS):
                half(0, c)
            with eng.Fori(1, HALVES // SLOTS - 1) as q:
                for c in range(SLOTS):
                    half(q, c)
            for c in range(SLOTS + 1):
                half(HALVES // SLOTS - 1, c)

        def run_groups(eng, group, n):
            group(0)
            with eng.Fori(1, n) as k:
                group(k)

        def w_part(n, low):
            which, k = n // 3, 2 * (n % 3)
            if which == 2:
                return (down_hi, down_lo)[low][:, k:k + 2, :]
            return ((up_hi, up_lo), (gate_hi, gate_lo))[which][low][:, :, k * P:(k + 2) * P]

        def w_bank(n):
            return banks[n % HG].rearrange("p (k n) -> p k n", k=2)

        def weights_due(i):
            w = -1 if i is None else i - TILES
            return range(3 * w, 3 * w + 3) if 0 <= w < 3 else range(0)

        def attn_w_part(n, low):
            return (wq_t[:, low], wkv_t[:, low, :, 0:D], wkv_t[:, low, :, D:2 * D], wo_t[:, low])[n]

        def attn_w_full(n):
            return wo_normed if n == 3 else banks[n].rearrange("p (k n) -> p k n", k=KD)

        block = ctx.enter_context(nc.Block())

        (S_X, C_X, S_UP, C_UP, S_GATE, C_GATE, S_SILU, C_SILU, S_PROD, C_PROD, S_OUT, S_SIG,
         T0, T1) = (scales[:, n:n + 1] for n in range(14))
        EXP = scales[:, 14:18].bitcast(I32)
        TO_F16, FROM_F16 = scales[:, 18:21], scales[:, 21:24]
        TO_F16_ATTN, FROM_F16_ATTN = scales[:, 24:28], scales[:, 28:32]
        Q, K, V, O = range(4)

        @block.sync
        def _(sp):
            sp.dma_start(idx_raw, x.rearrange("b (c p) -> (b c) p", p=P)).then_inc(x_loaded, 16)
            sp.dma_start(lora_b2[0:R, :], lora_b).then_inc(attn_w_loaded, 16)
            for n, w in enumerate((wq, wk, wv, wo)):
                sp.dma_start(attn_nat[:, n], w.rearrange("(k p) n -> p k n", p=P)).then_inc(attn_w_loaded, 16)
            for r in range(HG):
                sp.dma_start(norm_col[r * DH:(r + 1) * DH, :],
                             norm_w.rearrange("(d o) -> d o", o=1)).then_inc(attn_w_loaded, 16)
            for n, w in enumerate((w_up, w_gate, w_down)):
                width = KD * FF
                sp.dma_start(ffn_nat[:, n * width:(n + 1) * width].rearrange("p (k n) -> p k n", n=w.shape[1]),
                             w.rearrange("(k p) n -> p k n", p=P)).then_inc(ffn_w_loaded, 16)

            def iteration(g, u):
                c = u - 3
                if due(g, c):
                    tile_wait(sp, h2_ready, g, c)
                    sp.dma_start(h2_dram[at(g * GT + c, 1)].rearrange("o p d -> p (o d)"),
                                 h_all[:, at(g * GT + c, 1), :].rearrange("p o d -> p (o d)")
                                 ).then_inc(h2_stored[c % GT], 16)

            run_pipeline(sp, iteration)
            for n in range(GT):
                sp.wait_ge(h2_stored[n], 16 * (TILES // GT))

            out_v = out.rearrange("b (c p) d -> b p c d", p=P)

            def load(pair, s):
                sp.dma_start(res[:, s], h2_dram[at(pair * 2 * GT + s * GT, GT)].rearrange("t p d -> p t d")
                             ).then_inc(res_loaded[s], 16)

            def store(pair, s):
                for b in range(B):
                    sp.dma_start(out_v[b, :, at(pair * 4 + s * 2, 2), :],
                                 res[:, s].rearrange("p (c b) d -> p b c d", b=B)[:, b]
                                 ).then_inc(out_stored[s], 16)

            sp.wait_ge(prod_max, 2 * GROUPS)
            load(0, 0)
            load(0, 1)

            def pair_of_groups(q):
                for s in range(2):
                    sp.wait_ge(out_ready, q * (2 * GT) + (s + 1) * GT)
                    store(q, s)
                for s in range(2):
                    sp.wait_ge(out_stored[s], q * 32 + 32)
                    load(q + 1, s)

            with sp.Fori(0, GROUPS // 2 - 1) as q:
                pair_of_groups(q)
            last = GROUPS // 2 - 1
            for s in range(2):
                sp.wait_ge(out_ready, last * 2 * GT + (s + 1) * GT)
                store(last, s)
            for s in range(2):
                sp.wait_ge(out_stored[s], 32 * (GROUPS // 2))

        @block.gpsimd
        def _(pool):
            chain = [0]

            def link(ins):
                chain[0] += 1
                ins.then_inc(pool_chain, 1)
                pool.wait_ge(pool_chain, chain[0])

            link(pool.memset(ident[:], 0.0))
            pool.affine_select(out=ident[:], in_=ident[:], compare_op=ALU.not_equal, fill=1.0, base=0,
                               pattern=[[-1, P]], channel_multiplier=1).then_inc(ident_ready, 1)
            link(pool.memset(ones[:], 1.0))
            link(pool.memset(minus_half[:], -0.5))
            link(pool.memset(causal, 1.0))
            link(pool.affine_select(out=causal.rearrange("p (n t) -> p n t", t=P),
                                    in_=causal.rearrange("p (n t) -> p n t", t=P),
                                    compare_op=ALU.is_ge, fill=0.0, base=0, pattern=[[0, 2 * NG], [1, P]],
                                    channel_multiplier=-1))
            link(pool.memset(diag, 0.0))
            for r in range(HG):
                link(pool.memset(diag[r * DH:(r + 1) * DH, :, r * DV:(r + 1) * DV], 1.0))
            link(pool.memset(state, 0.0))
            pool.memset(v_ring, 1.0).then_inc(consts_ready, 1)

            def gather(n):
                for dst, table in ((base_ring, base), (lora_ring, lora_a)):
                    pool.indirect_dma_start(
                        dst[:, n], None, table,
                        bass.IndirectOffsetOnAxis(ap=idx_slot[:, n:n + 1], axis=0)).then_inc(gathered[n], 16)

            pool.wait_ge(idx_ready, 1)
            pool.tensor_copy(idx_slot[:], idx[:, 0:GT]).then_inc(slot_ready, GT)
            pool.wait_ge(slot_ready, GT)
            for n in range(GT):
                gather(n)

            def iteration(g, u):
                fetch = due(g, u) and due(g, u + GT)
                if fetch:
                    hold_on_constant(pool)
                    tile_wait(pool, h_ready, g, u)
                    tile_wait(pool, lora_turned, g, u)
                    pool.tensor_copy(idx_slot[:, u:u + 1], idx[:, at(g * GT + u + GT, 1)]).then_inc(slot_ready, 1)
                c = u + 1
                if due(g, c):
                    tile_wait(pool, vareps_ready, g, c)
                    if fetch:
                        tile_wait(pool, slot_ready, g, u + GT)
                    pool.tensor_tensor(rstd[:, c % 2, 0:1], vareps[:, c % 2, 0:1], minus_half[:, 0:1],
                                       ALU.pow).then_inc(rstd_ready, 1)
                c = u - 2
                if due(g, c):
                    tile_wait(pool, state_kept, g, c)
                    pool.tensor_tensor(state_new[:, c % 2], state_new[:, c % 2], diag, ALU.mult
                                       ).then_inc(state_masked, 1)
                    tile_wait(pool, state_masked, g, c)
                    pool.tensor_tensor(state[:, c % B], state[:, c % B], state_new[:, c % 2], ALU.add
                                       ).then_inc(state_ready, 1)
                    tile_wait(pool, meansq_ready, g, c)
                    pool.tensor_tensor(onorm[:, c % 2], meansq[:, c % 2], minus_half[:], ALU.pow
                                       ).then_inc(onorm_ready, 1)
                c = u - 3
                if due(g, c):
                    tile_wait(pool, vareps2_ready, g, c)
                    pool.tensor_tensor(rstd[:, c % 2, 1:2], vareps[:, c % 2, 1:2], minus_half[:, 0:1],
                                       ALU.pow).then_inc(rstd2_ready, 1)
                if fetch:
                    gather(u)

            run_pipeline(pool, iteration)

        @block.scalar
        def _(act):
            def copy(dst, src, scale=1.0):
                return act.activation(dst, src, ACT.Copy, scale=scale)

            act.wait_ge(attn_scales_ready, 1)
            for n in range(4):
                copy(attn_w_part(n, 0), attn_w_full(n), TO_F16_ATTN[:, n:n + 1]).then_inc(attn_w_hi, 1)
            act.wait_ge(consts_ready, 1)

            def two_blocks(bank, k=0):
                return bank[:, k * P:(k + KD) * P].rearrange("p (k n) -> p k n", k=KD)

            def iteration(g, u):
                for n in weights_due(GT * g + u - 1 if fixed(g) else None):
                    act.wait_ge(ffn_w_turned, n + 1)
                    copy(w_part(n, 0), w_bank(n)).then_inc(ffn_w_hi, 1)
                c = u
                if due(g, c):
                    tile_wait(act, kv_done, g, c)
                    copy(k_ring[:, c % GT], kv_bank[:, 0:D], FROM_F16_ATTN[:, K:K + 1]).then_inc(k_ready, 1)
                    copy(v_ring[:, c % GT, :, 0:DH], kv_bank[:, D:2 * D].rearrange("p (h d) -> p h d", h=H),
                         FROM_F16_ATTN[:, V:V + 1]).then_inc(v_ready, 1)
                    tile_wait(act, q_done, g, c)
                    copy(qkt_ring[:, c % GT, 0:NG], two_blocks(qws_bank), FROM_F16_ATTN[:, Q:Q + 1]
                         ).then_inc(q_t_ready, 1)
                c = u - 3
                if due(g, c):
                    tile_wait(act, o_turned, g, c)
                    copy(o_t[:, c % 2, 0], two_blocks(turn_bank), NORMED_TO_F16).then_inc(o_hi_ready, 1)
                c = u + 2
                if due(g, c):
                    tile_wait(act, lora_turned, g, c)
                    copy(lora_t[0:R, c % 2], turn_bank[0:R, KD * P:KD * P + P]).then_inc(lora_t_ready, 1)
                c = u
                if due(g, c):
                    tile_wait(act, k_turned, g, c)
                    copy(qkt_ring[:, c % GT, NG:2 * NG], two_blocks(kv_bank)).then_inc(k_t_ready, 1)
                c = u - 2
                if due(g, c):
                    tile_wait(act, state_done, g, c)
                    copy(state_new[:, c % 2], qws_bank[:, 0:NG * SW].rearrange("p (n w) -> p n w", n=NG)
                         ).then_inc(state_kept, 1)
                    tile_wait(act, o_done, g, c)
                    act.activation(squares[:, c % 2], lo_bank[:, 0:H * DV].rearrange(
                        "p (h d) -> p h d", h=H), ACT.Square).then_inc(squares_ready, 1)
                c = u + 1
                if due(g, c):
                    tile_wait(act, xn_turned, g, c)
                    copy(xn_t[:, c % 2, 0], two_blocks(turn_bank), NORMED_TO_F16).then_inc(xn_hi_ready, 1)
                c = u - 4
                if due(g, c):
                    hold_on_constant(act)
                    tile_wait(act, xn2_turned, g, c)
                    copy(xn2_t[:, :, at((g * GT + c) * P, P)], two_blocks(turn_bank, KD)
                         ).then_inc(xn2_t_ready, 1)

            run_pipeline(act, iteration)

            act.wait_ge(scale_ready, 1)

            def quantise_x(n, s):
                hold_on_constant(act)
                if not fixed(n) or n >= 2:
                    act.wait_ge(xl_ready, n - 1)
                copy(x16[:, s], xn2_t[:, :, at(n * GW, GW)], C_X).then_inc(x16_ready, 1)
                hold_on_constant(act)
                act.wait_ge(x16_ready, n + 1)
                copy(xh[:, :, at(n * GW, GW)], x16[:, s]).then_inc(xh_ready, 1)

            def keep(n, s, done, kept, also):
                for m in range(MF):
                    hold_on_constant(act)
                    act.wait_ge(done, n * MF + m + 1)
                    copy(big[:, at(n * GF + m * GW, GW)], banks[m]).then_inc(kept, 1)
                    if m == 1 and also is not None:
                        quantise_x(n + 1, s)

            quantise_x(0, 0)
            for n in range(GT):
                act.wait_ge(h2_stored[n], 16 * (TILES // GT))
            keep(0, 1, up_done, up_kept, True)
            keep(1, 0, up_done, up_kept, True)
            with act.Fori(1, GROUPS // 2 - 1) as q:
                for s in range(2):
                    keep(q * 2 + s, 1 - s, up_done, up_kept, True)
            keep(GROUPS - 2, 1, up_done, up_kept, True)
            keep(GROUPS - 1, 0, up_done, up_kept, None)

            def keep_gate(n):
                act.wait_ge(up_quantised, n + 1)
                keep(n, 0, gate_done, gate_kept, None)

            run_groups(act, keep_gate, GROUPS)

            act.activation(table_loader[:], ones[:, 0:1], ACT.Sigmoid)
            act.wait_ge(scale_ready, 3)

            def gate_half(q, s):
                def integers():
                    c = s + 1
                    hold_on_constant(act)
                    half_wait(act, silu_ready, q, c - SLOTS)
                    copy(g16[c % SLOTS], big[:, at((q * SLOTS + c) * HALF, HALF)], C_GATE
                         ).then_inc(gate_quantised, 1)

                first = fixed(q) and SLOTS * q + s == 0
                if half_due(q, s + 1) and not first:
                    integers()
                c = s
                if half_due(q, c):
                    hold_on_constant(act)
                    half_wait(act, gate_quantised, q, c)
                    act.activation(sig[:, c % SLOTS], g16[c % SLOTS], ACT.Sigmoid, scale=S_GATE
                                   ).then_inc(sig_ready, 1)
                if first:
                    integers()
                if steps_on_act(q, c):
                    half_wait(act, sig_ready, q, c)
                    copy(sig_steps[:, c % SLOTS], sig[:, c % SLOTS], SIG_STEPS).then_inc(steps_ready, 1)

            run_halves(act, gate_half)

            act.wait_ge(scale_ready, 4)

            def silu_half(q, s):
                c = s
                if half_due(q, c):
                    hold_on_constant(act)
                    half_wait(act, prod_ready, q, c - SLOTS)
                    copy(g16[c % SLOTS], big[:, at((q * SLOTS + c) * HALF, HALF)], C_SILU
                         ).then_inc(silu_quantised, 1)

            run_halves(act, silu_half)

            act.wait_ge(scale_ready, 5)

            def product_parts(q, s):
                for half in range(2):
                    c = 2 * s + half
                    ms = slice(half * MF // 2, (half + 1) * MF // 2)
                    hold_on_constant(act)
                    half_wait(act, ol_ready, q, c - SLOTS)
                    copy(o16[:, s, ms].rearrange("p m n -> p (m n)"),
                         big[:, at((q * SLOTS + c) * HALF, HALF)], C_PROD).then_inc(o16_ready, 1)
                    if half == 0 and (not fixed(q) or q >= 1):
                        act.wait_ge(down_done, q * (2 * GT) + (s - 1) * GT)
                    half_wait(act, o16_ready, q, c)
                    copy(oh[:, s, ms], o16[:, s, ms]).then_inc(oh_ready, 1)

            def product_pair(q):
                product_parts(q, 0)
                product_parts(q, 1)

            run_groups(act, product_pair, GROUPS // 2)


        @block.vector
        def _(dve):
            chain = [0]

            def link(ins):
                chain[0] += 1
                ins.then_inc(dve_chain, 1)
                dve.wait_ge(dve_chain, chain[0])

            barriers = [0]

            def pick_largest(n, bank):
                barriers[0] += 1
                dve.wait_ge(maxima_turned, barriers[0])
                link(dve.tensor_reduce(top[0:n, 0:1], bank[0:n, 0:P], AX.X, ALU.max))
                dve.tensor_scalar(pick[0:n, 0:n], ident[0:n, 0:n], top[0:n, 0:1], None, ALU.mult
                                  ).then_inc(pick_ready, 1)

            def spread_largest(values):
                dve.tensor_reduce(maxima[:, 0:1], values, AX.X, ALU.max).then_inc(maxima_ready, 1)
                pick_largest(1, turn_bank)
                dve.wait_ge(top_spread, barriers[0])
                return turn_bank[:, 0:1]

            def scale_of(largest, units, scale, inverse):
                if units is None:
                    link(dve.tensor_scalar(scale, largest, 1.0 / QMAX_ACT, MIN_SCALE, ALU.mult, ALU.max))
                    dve.reciprocal(inverse, scale).then_inc(scale_ready, 1)
                    return
                link(dve.tensor_scalar(T0, largest, units, 1.0 / QMAX_ACT, ALU.mult, ALU.mult))
                link(dve.tensor_scalar(scale, T0, MIN_SCALE, None, ALU.max))
                link(dve.reciprocal(T1, scale))
                dve.tensor_scalar(inverse, T1, units, None, ALU.mult).then_inc(scale_ready, 1)

            dve.wait_ge(x_loaded, 16)
            dve.tensor_copy(idx_rows, idx_raw).then_inc(idx_rows_ready, 1)
            dve.wait_ge(idx_turned, 1)
            dve.tensor_copy(idx[:].rearrange("p (c b) -> p b c", b=B),
                            turn_bank[:, 0:TILES].rearrange("p (b c) -> p b c", b=B)).then_inc(idx_ready, 1)

            dve.wait_ge(attn_w_loaded, 16 * (1 + 4 + HG))
            dve.tensor_scalar(lora_b2[0:R, :], lora_b2[0:R, :], LORA_SCALING, None, ALU.mult
                              ).then_inc(lora_b_ready, 1)
            dve.tensor_reduce(maxima[:, 0:3], attn_nat[:, 0:3], AX.XY, ALU.max, apply_absolute_value=True)
            dve.wait_ge(attn_w_turned, 4)
            dve.tensor_scalar(wo_normed, banks[3].rearrange("p (k n) -> p k n", k=KD), norm_col, None, ALU.mult
                              ).then_inc(wo_normed_ready, 1)
            dve.wait_ge(wo_normed_ready, 1)
            dve.tensor_reduce(maxima[:, 3:4], wo_normed, AX.XY, ALU.max, apply_absolute_value=True
                              ).then_inc(maxima_ready, 1)
            pick_largest(4, turn_bank)

            def powers_of_two(largest, least, to, back, back_also, read):
                n = to.shape[1]
                exp = EXP[:, 0:n]
                dve.tensor_scalar(to, largest, least, None, ALU.max).then_inc(read, 1)
                dve.wait_ge(read, 1)
                link(dve.tensor_scalar(exp, to.bitcast(I32), 0x7F800000, None, ALU.bitwise_and))
                link(dve.tensor_scalar(back, exp.bitcast(F32), 2.0**-14 * back_also, None, ALU.mult))
                link(dve.tensor_scalar(exp, to.bitcast(I32), 23, 0xFF, ALU.logical_shift_right,
                                       ALU.bitwise_xor))
                link(dve.tensor_scalar(exp, exp, 23, None, ALU.logical_shift_left))
                return dve.tensor_scalar(to, exp.bitcast(F32), 2.0**13, None, ALU.mult)

            dve.wait_ge(top_spread, 1)
            powers_of_two(turn_bank[:, 0:4], 1e-30, TO_F16_ATTN, FROM_F16_ATTN, 1.0 / NORMED_TO_F16,
                          attn_maxima_read).then_inc(attn_scales_ready, 1)
            for n in range(4):
                dve.wait_ge(attn_w_hi, n + 1)
                dve.scalar_tensor_tensor(out=attn_w_part(n, 1), in0=attn_w_full(n), scalar=TO_F16_ATTN[:, n:n + 1],
                                         in1=attn_w_part(n, 0), op0=ALU.mult, op1=ALU.subtract
                                         ).then_inc(attn_w_lo, 1)

            blocks = ffn_nat.rearrange("p (b q) -> p b q", q=QBLOCK)
            step, rstep, fstep = blk[:, 0], blk[:, 1], blk[:, 2]

            def block_maxima():
                dve.wait_ge(ffn_w_loaded, 16 * 3)
                link(dve.tensor_reduce(step, blocks, AX.X, ALU.max, apply_absolute_value=True))
                dve.tensor_reduce(maxima[:, 0:3], step.rearrange("p (w b) -> p w b", w=3), AX.X, ALU.max
                                  ).then_inc(maxima_ready, 1)

            def matrix_scales():
                dve.wait_ge(top_spread, 2)
                link(powers_of_two(banks[0][:, 0:3], MIN_SCALE * QMAX_W, TO_F16, FROM_F16, 1.0, ffn_maxima_read))
                link(dve.tensor_scalar(step, step, 1.0 / QMAX_W, MIN_SCALE, ALU.mult, ALU.max))
                for w in range(3):
                    part = slice(w * NBLK // 3, (w + 1) * NBLK // 3)
                    dve.tensor_scalar(fstep[:, part], step[:, part], TO_F16[:, w:w + 1], None, ALU.mult)
                link(dve.reciprocal(rstep, step))

            def times_step(w, s):
                mine = slice(w * NBLK // 3, (w + 1) * NBLK // 3)
                return dve.tensor_tensor(blocks[:, mine], blocks[:, mine],
                                         s[:, mine].unsqueeze(2).to_broadcast([P, NBLK // 3, QBLOCK]), ALU.mult)

            def rounded(w):
                link(times_step(w, rstep))
                link(dve.tensor_scalar(ffn_nat[:, w * KD * FF:(w + 1) * KD * FF],
                                       ffn_nat[:, w * KD * FF:(w + 1) * KD * FF], ROUNDER, -ROUNDER,
                                       ALU.add, ALU.add))

            weight_steps = {-1: block_maxima, 0: matrix_scales}
            for w in range(2):
                weight_steps[1 + w] = lambda w=w: rounded(w)
            dve.wait_ge(consts_ready, 1)

            def norm_sums(g, c, which, ready, done):
                hold_on_constant(dve)
                tile_wait(dve, ready, g, c)
                dve.bn_stats(stats6[:, which], h_all[:, at(g * GT + c, 1), :].rearrange("p o d -> p (o d)")
                             ).then_inc(done, 1)

            def norm_stats(g, c, which, sums, first, second):
                hold_on_constant(dve)
                tile_wait(dve, sums, g, c)
                dve.bn_aggr(meanvar[:, c % 2, which], stats6[:, which]).then_inc(first, 1)
                tile_wait(dve, first, g, c)
                dve.tensor_scalar(vareps[:, c % 2, which:which + 1], meanvar[:, c % 2, which, 1:2], NORM_EPS,
                                  None, ALU.add).then_inc(second, 1)

            def normed(g, c, which, dst, ready, done):
                tile_wait(dve, ready, g, c)
                dve.tensor_scalar(dst[:, c % 2:c % 2 + 1], h_all[:, at(g * GT + c, 1), :],
                                  meanvar[:, c % 2, which, 0:1], rstd[:, c % 2, which:which + 1],
                                  ALU.subtract, ALU.mult).then_inc(done, 1)

            def low_part(parts, c, ready):
                dve.scalar_tensor_tensor(out=parts[:, c % 2, 1], in0=turn_bank[:, 0:KD * P].rearrange(
                    "p (k n) -> p k n", k=KD), scalar=NORMED_TO_F16, in1=parts[:, c % 2, 0],
                    op0=ALU.mult, op1=ALU.subtract).then_inc(ready, 1)

            o_bank = lo_bank[:, 0:H * DV].rearrange("p (h d) -> p h d", h=H)

            def iteration(g, u):
                i = GT * g + u if fixed(g) else None
                for n in weights_due(None if i is None else i - 1):
                    dve.wait_ge(ffn_w_hi, n + 1)
                    dve.tensor_tensor(w_part(n, 1), w_bank(n), w_part(n, 0), ALU.subtract).then_inc(ffn_w_lo, 1)
                c = u - 3
                if due(g, c):
                    tile_wait(dve, onorm_ready, g, c)
                    dve.tensor_tensor(o_n[:, c % 2].rearrange("p (h d) -> p h d", h=H), o_bank[:, :, 0:DH],
                                      onorm[:, c % 2].unsqueeze(2).to_broadcast([P, H, DH]), ALU.mult
                                      ).then_inc(o_n_ready, 1)
                c = u - 4
                if due(g, c):
                    normed(g, c, 1, xn2, rstd2_ready, xn2_ready)
                c = u + 1
                if due(g, c):
                    slot_wait(dve, gathered[c % GT], g, c, 32)
                    tile_wait(dve, lora_done, g, c)
                    dve.tensor_tensor(h_all[:, at(g * GT + c, 1), :], base_ring[:, c % GT:c % GT + 1, :],
                                      lo_bank[:, 0:D].unsqueeze(1), ALU.add).then_inc(h_ready, 1)
                c = u - 3
                if due(g, c):
                    tile_wait(dve, o_hi_ready, g, c)
                    tile_wait(dve, lora_t_ready, g, u + 2)
                    low_part(o_t, c, o_lo_ready)
                c = u + 1
                if due(g, c):
                    norm_sums(g, c, 0, h_ready, stats_done)
                c = u - 5
                if due(g, c):
                    hold_on_constant(dve)
                    tile_wait(dve, xn2_t_ready, g, c)
                    dve.tensor_reduce(absmax[:, at(g * GT + c, 1)], xn2_t[:, :, at((g * GT + c) * P, P)],
                                      AX.XY, ALU.max, apply_absolute_value=True).then_inc(absmax_ready, 1)
                c = u + 1
                if due(g, c):
                    norm_stats(g, c, 0, stats_done, meanvar_done, vareps_ready)
                if i == 0:
                    pick_largest(3, banks[0])

                def mask_scores(half):
                    r = slice(2 * half, 2 * half + 2)
                    dve.tensor_tensor(probs[:, (u - 1) % 2, r].rearrange("p r n t -> p r (n t)"),
                                      scores_ps[:, r, 0:NG * P], causal.rearrange("p (r n) -> p r n", r=2),
                                      ALU.mult).then_inc(probs_ready, 1)

                c = u - 1
                if due(g, c):
                    tile_wait(dve, scores_done, g, c)
                    mask_scores(0)
                c = u + 1
                if due(g, c):
                    normed(g, c, 0, xn, rstd_ready, xn_ready)
                c = u - 1
                if due(g, c):
                    mask_scores(1)
                if i == TILES + 1:
                    rounded(2)
                elif i in (TILES - 1, TILES, TILES + 2):
                    times_step(min(i - (TILES - 1), 2), fstep).then_inc(ffn_w_quantised, 1)
                c = u - 2
                if due(g, c):
                    tile_wait(dve, squares_ready, g, c)
                    dve.tensor_scalar(denom2[:].unsqueeze(2), squares[:, c % 2, :, DH:DV], 1.0, NORM_EPS,
                                      ALU.max, ALU.mult).then_inc(denom2_done, 1)
                    dve.tensor_reduce(ssq[:], squares[:, c % 2, :, 0:DH], AX.X, ALU.add).then_inc(ssq_done, 1)
                    tile_wait(dve, ssq_done, g, c)
                    tile_wait(dve, denom2_done, g, c)
                    dve.scalar_tensor_tensor(out=meansq[:, c % 2], in0=ssq[:], scalar=1.0 / DH, in1=denom2[:],
                                             op0=ALU.mult, op1=ALU.add).then_inc(meansq_ready, 1)
                c = u + 1
                if due(g, c):
                    tile_wait(dve, xn_hi_ready, g, c)
                    tile_wait(dve, xn2_t_ready, g, u - 4)
                    low_part(xn_t, c, xn_lo_ready)
                c = u - 3
                if due(g, c):
                    tile_wait(dve, attn_done, g, c)
                    dve.scalar_tensor_tensor(out=h_all[:, at(g * GT + c, 1), :], in0=qws_bank[:, 0:D].unsqueeze(1),
                                             scalar=FROM_F16_ATTN[:, O:O + 1], in1=h_all[:, at(g * GT + c, 1), :],
                                             op0=ALU.mult, op1=ALU.add).then_inc(h2_ready, 1)
                    norm_sums(g, c, 1, h2_ready, stats2_done)
                    norm_stats(g, c, 1, stats2_done, meanvar2_done, vareps2_ready)
                if i in weight_steps:
                    weight_steps[i]()

            run_pipeline(dve, iteration)

            dve.wait_ge(absmax_ready, TILES)
            largest = spread_largest(absmax[:, 0:TILES])
            scale_of(largest, None, S_X, C_X)

            def low_x(n, s):
                dve.wait_ge(xh_ready, n + 1)
                dve.tensor_tensor(xl[:, :, at(n * GW, GW)], x16[:, s], xh[:, :, at(n * GW, GW)], ALU.subtract
                                  ).then_inc(xl_ready, 1)

            def group_max(n, kept, done, pieces=(3, 3)):
                k = 0
                for piece in pieces:
                    hold_on_constant(dve)
                    dve.wait_ge(kept, n * MF + (k + piece))
                    dve.tensor_reduce(absmax[:, at(n * MF + k, piece)],
                                      big[:, at(n * GF + k * GW, piece * GW)].rearrange("p (m n) -> p m n", m=piece),
                                      AX.X, ALU.max, apply_absolute_value=True).then_inc(done, 1)
                    k += piece

            last_pieces = (3, 2, 1)

            low_x(0, 0)
            low_x(1, 1)
            group_max(0, up_kept, up_max)
            low_x(2, 0)
            group_max(1, up_kept, up_max)
            with dve.Fori(1, GROUPS // 2 - 1) as q:
                for s in range(2):
                    low_x(q * 2 + (s + 1), 1 - s)
                    group_max(q * 2 + s, up_kept, up_max)
            low_x(GROUPS - 1, 1)
            group_max(GROUPS - 2, up_kept, up_max)
            group_max(GROUPS - 1, up_kept, up_max, last_pieces)
            dve.wait_ge(up_max, 2 * GROUPS + 1)
            largest = spread_largest(absmax[:])
            link(dve.tensor_scalar(S_PROD, S_X, FROM_F16[:, 0:1], None, ALU.mult))
            scale_of(largest, S_PROD, S_UP, C_UP)
            dve.wait_ge(scale_ready, 2)

            def quantise_up(n):
                dve.tensor_scalar(quant[:, at(n * GF, GF)], big[:, at(n * GF, GF)], C_UP, None, ALU.mult
                                  ).then_inc(up_quantised, 1)

            def up_and_gate(n):
                quantise_up(n)
                group_max(n, gate_kept, gate_max)

            run_groups(dve, up_and_gate, GROUPS - 1)
            quantise_up(GROUPS - 1)
            group_max(GROUPS - 1, gate_kept, gate_max, last_pieces)
            dve.wait_ge(gate_max, 2 * GROUPS + 1)
            largest = spread_largest(absmax[:])
            link(dve.tensor_scalar(S_PROD, S_X, FROM_F16[:, 1:2], None, ALU.mult))
            scale_of(largest, S_PROD, S_GATE, C_GATE)
            dve.wait_ge(scale_ready, 3)
            link(dve.tensor_scalar(S_SIG, S_GATE, 1.0 / SIG_STEPS, None, ALU.mult))

            def half_max(q, c, ready, done):
                hold_on_constant(dve)
                half_wait(dve, ready, q, c)
                dve.tensor_reduce(absmax[:, at(q * SLOTS + c, 1)], big[:, at((q * SLOTS + c) * HALF, HALF)], AX.X,
                                  ALU.max, apply_absolute_value=True).then_inc(done, 1)

            def silu_half(q, s):
                c = s
                mine = half_due(q, c) and not steps_on_act(q, c)
                if mine:
                    half_wait(dve, sig_ready, q, c)
                    slot = (c + 1) // 2 % 2
                    dve.tensor_scalar(sig16[:, slot], sig[:, c], SIG_STEPS, QMAX_SIG, ALU.mult, ALU.min
                                      ).then_inc(sig_quantised, 1)
                if half_due(q, c - 1):
                    half_max(q, c - 1, silu_ready, silu_max)
                if half_due(q, c):
                    dst = big[:, at((q * SLOTS + c) * HALF, HALF)]
                    if mine:
                        dve.wait_ge(sig_quantised, q * (SLOTS // 2) + ((c + 1) // 2 + 1))
                        dve.tensor_tensor(dst, sig16[:, slot], g16[c], ALU.mult).then_inc(silu_ready, 1)
                    else:
                        dve.wait_ge(steps_ready, q * (SLOTS // 2) + (c // 2 + 1))
                        dve.scalar_tensor_tensor(out=dst, in0=sig_steps[:, c], scalar=QMAX_SIG, in1=g16[c],
                                                 op0=ALU.min, op1=ALU.mult).then_inc(silu_ready, 1)

            run_halves(dve, silu_half)
            dve.wait_ge(silu_max, 2 * GROUPS)
            largest = spread_largest(absmax[:, 0:HALVES])
            scale_of(largest, S_SIG, S_SILU, C_SILU)

            def product_half(q, s):
                c = s
                if half_due(q, c):
                    half_wait(dve, silu_quantised, q, c)
                    dve.tensor_tensor(big[:, at((q * SLOTS + c) * HALF, HALF)], g16[c],
                                      quant[:, at((q * SLOTS + c) * HALF, HALF)], ALU.mult
                                      ).then_inc(prod_ready, 1)
                if half_due(q, c - 1):
                    half_max(q, c - 1, prod_ready, prod_max)

            run_halves(dve, product_half)
            dve.wait_ge(prod_max, 2 * GROUPS)
            largest = spread_largest(absmax[:, 0:HALVES])
            dve.wait_ge(scale_ready, 4)
            link(dve.tensor_scalar(T1, S_SILU, S_UP, None, ALU.mult))
            link(dve.tensor_copy(S_SIG, T1))
            scale_of(largest, S_SIG, S_PROD, C_PROD)
            dve.wait_ge(scale_ready, 5)
            link(dve.tensor_scalar(S_OUT, S_PROD, FROM_F16[:, 2:3], None, ALU.mult))

            def low_product(q, s):
                for half in range(2):
                    ms = slice(half * MF // 2, (half + 1) * MF // 2)
                    half_wait(dve, oh_ready, q, 2 * s + half)
                    dve.tensor_tensor(ol[:, s % 2, ms], o16[:, s % 2, ms], oh[:, s % 2, ms], ALU.subtract
                                      ).then_inc(ol_ready, 1)

            def finish(q, s):
                dve.wait_ge(res_loaded[s], q * 16 + 16)
                for t in range(GT):
                    dve.wait_ge(down_done, q * (2 * GT) + (s * GT + t + 1))
                    dve.scalar_tensor_tensor(out=res[:, s, t], in0=banks[(s * GT + t) % 8][:, 0:D],
                                             scalar=S_OUT, in1=res[:, s, t], op0=ALU.mult, op1=ALU.add
                                             ).then_inc(out_ready, 1)

            low_product(0, 0)
            with dve.Fori(0, GROUPS // 2 - 1) as q:
                for s in range(2):
                    low_product(q, s + 1)
                    finish(q, s)
            low_product(GROUPS // 2 - 1, 1)
            finish(GROUPS // 2 - 1, 0)
            finish(GROUPS // 2 - 1, 1)

        @block.tensor
        def _(pe):
            barriers = [0]

            def turn_maxima(n, bank):
                barriers[0] += 1
                pe.wait_ge(maxima_ready, barriers[0])
                pe.transpose(bank[0:n, 0:P], maxima[:, 0:n], ident[:]).then_inc(maxima_turned, 1)

            def spread_pick(n, bank):
                pe.wait_ge(pick_ready, barriers[0])
                pe.matmul(bank[:, 0:n], ones[0:n, :], pick[0:n, 0:n], start=True, stop=True
                          ).then_inc(top_spread, 1)

            def spread_largest():
                turn_maxima(1, turn_bank)
                spread_pick(1, turn_bank)

            pe.wait_ge(ident_ready, 1)
            pe.wait_ge(idx_rows_ready, 1)
            pe.transpose(turn_bank[:, 0:TILES], idx_rows, ident[0:TILES, 0:TILES]).then_inc(idx_turned, 1)
            pe.wait_ge(attn_w_loaded, 16 * (1 + 4 + HG))
            for n in range(4):
                for k in range(KD):
                    for o in range(OT):
                        last = pe.transpose(banks[n][:, k * D + o * P:k * D + (o + 1) * P],
                                            attn_nat[:, n, o, k * P:(k + 1) * P], ident[:])
                last.then_inc(attn_w_turned, 1)
            pe.wait_ge(consts_ready, 1)
            pe.wait_ge(idx_ready, 1)
            turn_maxima(4, turn_bank)
            spread_pick(4, turn_bank)

            def turn_weights(n):
                which, k0 = n // 3, 2 * (n % 3)
                nat = ffn_nat[:, which * KD * FF:(which + 1) * KD * FF]
                for a in range(2):
                    for b in range(2):
                        if which < 2:
                            src = nat.rearrange("p (o n) -> p o n", n=D)[:, k0 + b, a * P:(a + 1) * P]
                        else:
                            src = nat.rearrange("p (o n) -> p o n", n=FF)[:, b, (k0 + a) * P:(k0 + a + 1) * P]
                        last = pe.transpose(w_bank(n)[:, a, b * P:(b + 1) * P], src, ident[:])
                last.then_inc(ffn_w_turned, 1)

            pe.wait_ge(lora_b_ready, 1)
            pe.wait_ge(idx_ready, 1)
            pe.wait_ge(attn_maxima_read, 1)

            def iteration(g, u):
                i = GT * g + u if fixed(g) else None
                if i == 0:
                    pe.wait_ge(attn_w_lo, 4)
                c = u
                if due(g, c):
                    x_t = xn_t[:, c % 2]
                    tile_wait(pe, xn_hi_ready, g, c)
                    tile_wait(pe, k_t_ready, g, c - 1)
                    for k in range(KD):
                        pe.matmul(kv_bank[:], x_t[:, 0, k], wkv_t[:, 0, k], start=(k == 0), stop=False)
                        pe.matmul(kv_bank[:], x_t[:, 0, k], wkv_t[:, 1, k], start=False, stop=False)
                    tile_wait(pe, xn_lo_ready, g, c)
                    for k in range(KD):
                        last = pe.matmul(kv_bank[:], x_t[:, 1, k], wkv_t[:, 0, k], start=False,
                                         stop=(k == KD - 1))
                    last.then_inc(kv_done, 1)
                    tile_wait(pe, h2_ready, g, u - 4)
                    if fixed(g):
                        tile_wait(pe, state_kept, g, u - 3)
                        tile_wait(pe, q_t_ready, g, u - 1)
                    for n in range(NG):
                        cols = slice(n * P, (n + 1) * P)
                        for k in range(KD):
                            first = n == 0 and k == 0
                            pe.matmul(qws_bank[:, cols], wq_t[:, 0, k, cols], x_t[:, 0, k], start=first, stop=False,
                                      skip_group_check=True)
                            pe.matmul(qws_bank[:, cols], wq_t[:, 1, k, cols], x_t[:, 0, k], start=False, stop=False,
                                      skip_group_check=True)
                            last = pe.matmul(qws_bank[:, cols], wq_t[:, 0, k, cols], x_t[:, 1, k], start=False,
                                             stop=(k == KD - 1), skip_group_check=True)
                    last.then_inc(q_done, 1)
                if i == 0:
                    turn_maxima(3, banks[0])

                def scores(n):
                    tile_wait(pe, k_t_ready, g, u - 1)
                    tile_wait(pe, probs_ready, g, u - 2, 2)
                    if i == 1:
                        pe.wait_ge(ffn_maxima_read, 1)
                    for r in range(HG):
                        rows = slice(r * DH, (r + 1) * DH)
                        last = pe.matmul(scores_ps[:, r, n * P:(n + 1) * P], qkt_ring[rows, (u - 1) % GT, NG + n],
                                         qkt_ring[rows, (u - 1) % GT, n], start=True, stop=True)
                    if n == NG - 1:
                        last.then_inc(scores_done, 1)

                if due(g, u - 1):
                    scores(0)
                if i == TILES:
                    scores(1)

                def free_turn_bank():
                    tile_wait(pe, xn_lo_ready, g, u)
                    if fixed(g):
                        tile_wait(pe, xn2_t_ready, g, u - 5)
                        tile_wait(pe, lora_t_ready, g, u + 1)
                        tile_wait(pe, o_lo_ready, g, u - 4)

                c = u + 2
                if due(g, c):
                    hold_on_constant(pe)
                    slot_wait(pe, gathered[c % GT], g, c, 32)
                    free_turn_bank()
                    pe.transpose(turn_bank[0:R, KD * P:KD * P + P], lora_ring[:, c % GT], ident[:]
                                 ).then_inc(lora_turned, 1)
                c = u - 3
                if due(g, c):
                    tile_wait(pe, o_n_ready, g, c)
                    free_turn_bank()
                    for k in range(KD):
                        last = pe.transpose(turn_bank[:, k * P:(k + 1) * P], o_n[:, c % 2, k * P:(k + 1) * P],
                                            ident[:])
                    last.then_inc(o_turned, 1)
                c = u + 1
                if due(g, c):
                    tile_wait(pe, lora_t_ready, g, c)
                    tile_wait(pe, o_n_ready, g, u - 3)
                    if fixed(g):
                        tile_wait(pe, h_ready, g, u)
                    pe.matmul(lo_bank[:, 0:D], lora_t[0:R, c % 2], lora_b2[0:R, :], start=True, stop=True
                              ).then_inc(lora_done, 1)
                if i == 0:
                    spread_pick(3, banks[0])
                if due(g, u - 1) and i != TILES:
                    scores(1)
                c = u
                if due(g, c):
                    tile_wait(pe, v_ready, g, c)
                    for n in range(NG):
                        last = pe.transpose(kv_bank[:, n * P:(n + 1) * P], k_ring[:, c % GT, n * P:(n + 1) * P],
                                            ident[:])
                    last.then_inc(k_turned, 1)
                c = u - 2
                if due(g, c):
                    tile_wait(pe, state_ready, g, u - 4)
                    tile_wait(pe, h_ready, g, u + 1)
                    if fixed(g):
                        tile_wait(pe, o_n_ready, g, u - 3)
                    for n in range(NG):
                        pe.matmul(lo_bank[:, n * SW:(n + 1) * SW], qkt_ring[:, c % GT, n], state[:, c % B, n],
                                  start=(n == 0), stop=False, skip_group_check=True)
                    tile_wait(pe, q_t_ready, g, u)
                    if fixed(g):
                        tile_wait(pe, h2_ready, g, u - 4)
                    for n in range(NG):
                        last = pe.matmul(qws_bank[:, n * SW:(n + 1) * SW], k_ring[:, c % GT, n * P:(n + 1) * P],
                                         v_ring[:, c % GT, n * HG:(n + 1) * HG].rearrange("p h d -> p (h d)"),
                                         start=(n == 0), stop=(n == NG - 1), skip_group_check=True)
                    last.then_inc(state_done, 1)
                    tile_wait(pe, probs_ready, g, c, 2)
                    for h in range(H):
                        last = pe.matmul(lo_bank[:, h * DV:(h + 1) * DV], probs[:, c % 2, h % HG, h // HG],
                                         v_ring[:, c % GT, h], start=False, stop=(h == H - 1),
                                         skip_group_check=True)
                    last.then_inc(o_done, 1)

                def turn_bank_read():
                    tile_wait(pe, o_lo_ready, g, u - 3)
                    if fixed(g):
                        tile_wait(pe, lora_t_ready, g, u + 2)
                        tile_wait(pe, xn_lo_ready, g, u)
                        tile_wait(pe, xn2_t_ready, g, u - 5)

                c = u - 4
                if due(g, c):
                    tile_wait(pe, xn2_ready, g, c)
                    turn_bank_read()
                    for k in range(KD):
                        last = pe.transpose(turn_bank[:, (KD + k) * P:(KD + k + 1) * P],
                                            xn2[:, c % 2, k * P:(k + 1) * P], ident[:])
                    last.then_inc(xn2_turned, 1)
                c = u + 1
                if due(g, c):
                    tile_wait(pe, xn_ready, g, c)
                    turn_bank_read()
                    for k in range(KD):
                        last = pe.transpose(turn_bank[:, k * P:(k + 1) * P], xn[:, c % 2, k * P:(k + 1) * P],
                                            ident[:])
                    last.then_inc(xn_turned, 1)
                c = u - 3
                if due(g, c):
                    tile_wait(pe, o_lo_ready, g, c)
                    tile_wait(pe, state_kept, g, u - 2)
                    if fixed(g):
                        tile_wait(pe, h2_ready, g, u - 4)
                    for k in range(KD):
                        for a, b in ((0, 0), (0, 1), (1, 0)):
                            last = pe.matmul(qws_bank[:, 0:D], o_t[:, c % 2, a, k], wo_t[:, b, k],
                                             start=(k == 0 and a + b == 0), stop=(k == KD - 1 and a == 1))
                    last.then_inc(attn_done, 1)
                for n in weights_due(i):
                    pe.wait_ge(ffn_w_quantised, n // 3 + 1)
                    pe.wait_ge(probs_ready, 2 * TILES)
                    if n >= HG:
                        pe.wait_ge(ffn_w_lo, n - HG + 1)
                    turn_weights(n)

            run_pipeline(pe, iteration)

            def project(n, m, hi, lo, done, low_x=None):
                cols = slice(m * P, (m + 1) * P)
                xs = at(n * GW, GW)
                for k in range(KD):
                    pe.matmul(banks[m], hi[:, k, cols], xh[:, k, xs], start=(k == 0), stop=False)
                    pe.matmul(banks[m], lo[:, k, cols], xh[:, k, xs], start=False, stop=False)
                if low_x is not None:
                    pe.wait_ge(low_x, n + 1)
                for k in range(KD):
                    last = pe.matmul(banks[m], hi[:, k, cols], xl[:, k, xs], start=False, stop=(k == KD - 1))
                last.then_inc(done, 1)

            spread_largest()
            pe.wait_ge(ffn_w_lo, 9)

            def up_group(n):
                pe.wait_ge(xh_ready, n + 1)
                for m in range(MF):
                    if not fixed(n) or n >= 1:
                        pe.wait_ge(up_kept, n * MF + (m + 1 - MF))
                    project(n, m, up_hi, up_lo, up_done, xl_ready if m == 0 else None)

            run_groups(pe, up_group, GROUPS)

            def gate_group(n):
                for m in range(MF):
                    if fixed(n) and n == 0:
                        pe.wait_ge(up_kept, (GROUPS - 1) * MF + m + 1)
                    else:
                        pe.wait_ge(gate_kept, n * MF + (m + 1 - MF))
                    project(n, m, gate_hi, gate_lo, gate_done)
                    if fixed(n) and m == 1:
                        spread_largest()

            run_groups(pe, gate_group, GROUPS)
            for _ in range(3):
                spread_largest()
            pe.wait_ge(gate_kept, GROUPS * MF)
            pe.wait_ge(scale_ready, 5)

            def down_pair(q):
                for s in range(2):
                    for half in range(2):
                        ms = range(half * MF // 2, (half + 1) * MF // 2)
                        half_wait(pe, oh_ready, q, 2 * s + half)
                        for t in range(GT):
                            bank = banks[s * GT + t][:, 0:D]
                            if half == 0 and (not fixed(q) or q >= 1):
                                pe.wait_ge(out_ready, q * (2 * GT) + (s * GT + t + 1 - 2 * GT))
                            for m in ms:
                                high = oh[:, s, m, t * P:(t + 1) * P]
                                pe.matmul(bank, high, down_hi[:, m], start=(m == 0), stop=False)
                                pe.matmul(bank, high, down_lo[:, m], start=False, stop=False)
                        half_wait(pe, ol_ready, q, 2 * s + half)
                        for t in range(GT):
                            bank = banks[s * GT + t][:, 0:D]
                            for m in ms:
                                last = pe.matmul(bank, ol[:, s, m, t * P:(t + 1) * P], down_hi[:, m], start=False,
                                                 stop=(m == MF - 1))
                            if half:
                                last.then_inc(down_done, 1)

            run_groups(pe, down_pair, GROUPS // 2)


_INS = ["x", "L0_tok_base_weight", "L0_tok_lora_A", "L0_tok_lora_B", "L0_attn_Wq", "L0_attn_Wk", "L0_attn_Wv",
        "L0_attn_Wo", "L0_attn_norm_w", "L0_ffn_w_gate", "L0_ffn_w_up", "L0_ffn_w_down"]


def kernel(**inputs):
    import numpy as _np
    import concourse.bacc as _bacc
    from concourse import mybir as _mybir
    from concourse.bass_utils import run_bass_kernel_spmd as _run

    nc = _bacc.Bacc("TRN2", target_bir_lowering=False, num_devices=1)
    arrays, args = {}, []
    for name in _INS:
        a = _np.ascontiguousarray(inputs[name])
        arrays[f"in_{name}"] = a
        args.append(nc.dram_tensor(f"in_{name}", a.shape, _mybir.dt.from_np(a.dtype), kind="ExternalInput").ap())
    batch, length = inputs["x"].shape
    width = inputs["L0_tok_base_weight"].shape[1]
    args.append(nc.dram_tensor("out_h", (batch, length, width), _mybir.dt.float32, kind="ExternalOutput").ap())
    lm_tower(nc, *args)
    r = _run(nc, [arrays], core_ids=[0])
    return r.results[0]["out_h"]
```
